# Optimizing a Trainium2 kernel written in Bass

```python
import numpy as np
import jax
import jax.numpy as jnp

def _softmax(x, axis=-1):
    return jax.nn.softmax(x, axis=axis)

def _gelu(x):
    return jax.nn.gelu(x, approximate=True)

def _silu(x):
    return jax.nn.silu(x)

def _sigmoid(x):
    return jax.nn.sigmoid(x)

def _layernorm(x, axis=-1, eps=1e-05):
    m = jnp.mean(x, axis=axis, keepdims=True)
    v = jnp.var(x, axis=axis, keepdims=True)
    return (x - m) / jnp.sqrt(v + eps)

def _scatter_add(tgt, idx, src, axis=0):
    return tgt.at[idx].add(src)

def _segment_sum(src, seg, n):
    return jax.ops.segment_sum(src, seg, n)
kernel_name = 'mk_cond_resid_d4_seqx_r8_e73d13'

def setup_inputs(seed: int=0):
    np.random.seed(seed)
    _w = jnp.asarray

    def _rec_inputs():
        import jax
        import jax.numpy as jnp
        _rk = jax.random.key(seed)
        x = 2.818e-05 + 1 * jax.random.normal(jax.random.fold_in(_rk, 1), (64, 32, 128), jnp.float32)
        _lenS = 32 - jax.random.randint(jax.random.fold_in(_rk, 7), (64,), 0, max(1, 32 // 4) + 1, jnp.int32)
        _lenS2 = 32 - jax.random.randint(jax.random.fold_in(_rk, 8), (64,), 0, max(1, 32 // 4) + 1, jnp.int32)
        cond_1024 = 0.00185052 + 1.01138 * jax.random.normal(jax.random.fold_in(_rk, 11), (64, 128), jnp.float32)
        return (x, cond_1024)
    x, cond_1024 = _rec_inputs()

    def _L0_cond_setup():
        import jax, jax.numpy as jnp
        import numpy as np
        D = 128
        key = jax.random.key(seed)
        ks = jax.random.split(key, 12)
        sc_in = 1.0 / np.sqrt(D)
        sc_in2 = 1.0 / np.sqrt(2 * D)
        inp = {'X1': jax.random.normal(ks[0], (8, D), dtype=jnp.float32), 'X2': jax.random.normal(ks[1], (8, 256, D), dtype=jnp.float32), 'Wq1': jax.random.normal(ks[2], (D, D), dtype=jnp.float32) * sc_in, 'bq1': jax.random.normal(ks[3], (D,), dtype=jnp.float32) * 0.01, 'Wq2': jax.random.normal(ks[4], (D, D), dtype=jnp.float32) * sc_in, 'bq2': jax.random.normal(ks[5], (D,), dtype=jnp.float32) * 0.01, 'Wk1': jax.random.normal(ks[6], (D, D), dtype=jnp.float32) * sc_in, 'bk1': jax.random.normal(ks[7], (D,), dtype=jnp.float32) * 0.01, 'Wk2': jax.random.normal(ks[8], (D, D), dtype=jnp.float32) * sc_in, 'bk2': jax.random.normal(ks[9], (D,), dtype=jnp.float32) * 0.01, 'Wv': jax.random.normal(ks[10], (2 * D, D), dtype=jnp.float32) * sc_in2, 'bv': jax.random.normal(ks[11], (D,), dtype=jnp.float32) * 0.01, 'alpha': jnp.float32(0.5)}
        return inp
    _L0_cond_all = _L0_cond_setup()
    _L0_cond_in = {k: v for k, v in _L0_cond_all.items() if k in ('Wq1', 'bq1', 'Wq2', 'bq2', 'Wk1', 'bk1', 'Wk2', 'bk2', 'Wv', 'bv', 'alpha')}
    del _L0_cond_all

    def _L1_cond_setup():
        import jax, jax.numpy as jnp
        import numpy as np
        N, T, D, H = (64, 64, 128, 128)

        def lstm_scan(x, h0, Wx, Wh, b):
            xW = jnp.einsum('ntd,dg->ntg', x, Wx) + b
            Hdim = h0.shape[1]
            c0 = jnp.zeros_like(h0)

            def step(carry, xw_t):
                prev_h, prev_c = carry
                a = xw_t + prev_h @ Wh
                i = jax.nn.sigmoid(a[:, :Hdim])
                f = jax.nn.sigmoid(a[:, Hdim:2 * Hdim])
                o = jax.nn.sigmoid(a[:, 2 * Hdim:3 * Hdim])
                g = jnp.tanh(a[:, 3 * Hdim:])
                next_c = f * prev_c + i * g
                next_h = o * jnp.tanh(next_c)
                return ((next_h, next_c), next_h)
            _, hs = jax.lax.scan(step, (h0, c0), jnp.swapaxes(xW, 0, 1))
            return jnp.swapaxes(hs, 0, 1)
        key = jax.random.key(seed)
        k1, k2, k3, k4 = jax.random.split(key, 4)
        x = jax.random.normal(k1, (N, T, D), dtype=jnp.float32)
        h0 = jax.random.normal(k2, (N, H), dtype=jnp.float32)
        Wx = jax.random.normal(k3, (D, 4 * H), dtype=jnp.float32) / np.sqrt(D)
        Wh = jax.random.normal(k4, (H, 4 * H), dtype=jnp.float32) / np.sqrt(H)
        b = jnp.zeros((4 * H,), dtype=jnp.float32)
        return {'x': x, 'h0': h0, 'Wx': Wx, 'Wh': Wh, 'b': b}
    _L1_cond_all = _L1_cond_setup()
    _L1_cond_in = {k: v for k, v in _L1_cond_all.items() if k in ('Wx', 'Wh', 'b')}
    del _L1_cond_all

    def _L2_cond_setup():
        import jax, jax.numpy as jnp
        import numpy as np
        N, T, D, H = (128, 64, 128, 128)
        key = jax.random.key(seed)
        k1, k2, k3, k4 = jax.random.split(key, 4)
        x = jax.random.normal(k1, (N, T, D), dtype=jnp.float32)
        h0 = jax.random.normal(k2, (N, H), dtype=jnp.float32)
        Wx = jax.random.normal(k3, (D, H), dtype=jnp.float32) / np.sqrt(D)
        Wh = jax.random.normal(k4, (H, H), dtype=jnp.float32) / np.sqrt(H)
        b = jnp.zeros((H,), dtype=jnp.float32)
        return {'x': x, 'h0': h0, 'Wx': Wx, 'Wh': Wh, 'b': b}
    _L2_cond_all = _L2_cond_setup()
    _L2_cond_in = {k: v for k, v in _L2_cond_all.items() if k in ('Wx', 'Wh', 'b')}
    del _L2_cond_all

    def _L3_cond_setup():
        import jax, jax.numpy as jnp
        import numpy as np
        key = jax.random.key(seed)
        k1, k2, k3, k4 = jax.random.split(key, 4)
        N, T, D, H = (64, 64, 128, 128)
        x = jax.random.normal(k1, (N, T, D), dtype=jnp.float32)
        h0 = jax.random.normal(k2, (N, H), dtype=jnp.float32)
        Wx = jax.random.normal(k3, (D, 4 * H), dtype=jnp.float32) / np.sqrt(D)
        Wh = jax.random.normal(k4, (H, 4 * H), dtype=jnp.float32) / np.sqrt(H)
        b = jnp.zeros((4 * H,), dtype=jnp.float32)
        return {'x': x, 'h0': h0, 'Wx': Wx, 'Wh': Wh, 'b': b}
    _L3_cond_all = _L3_cond_setup()
    _L3_cond_in = {k: v for k, v in _L3_cond_all.items() if k in ('Wx', 'Wh', 'b')}
    del _L3_cond_all
    return {'x': x, 'cond_1024': cond_1024, 'L0_cond_Wq1': _L0_cond_in['Wq1'], 'L0_cond_bq1': _L0_cond_in['bq1'], 'L0_cond_Wq2': _L0_cond_in['Wq2'], 'L0_cond_bq2': _L0_cond_in['bq2'], 'L0_cond_Wk1': _L0_cond_in['Wk1'], 'L0_cond_bk1': _L0_cond_in['bk1'], 'L0_cond_Wk2': _L0_cond_in['Wk2'], 'L0_cond_bk2': _L0_cond_in['bk2'], 'L0_cond_Wv': _L0_cond_in['Wv'], 'L0_cond_bv': _L0_cond_in['bv'], 'L0_cond_alpha': _L0_cond_in['alpha'], 'L1_cond_Wx': _L1_cond_in['Wx'], 'L1_cond_Wh': _L1_cond_in['Wh'], 'L1_cond_b': _L1_cond_in['b'], 'L2_cond_Wx': _L2_cond_in['Wx'], 'L2_cond_Wh': _L2_cond_in['Wh'], 'L2_cond_b': _L2_cond_in['b'], 'L3_cond_Wx': _L3_cond_in['Wx'], 'L3_cond_Wh': _L3_cond_in['Wh'], 'L3_cond_b': _L3_cond_in['b']}

def reference(x, cond_1024, L0_cond_Wq1, L0_cond_bq1, L0_cond_Wq2, L0_cond_bq2, L0_cond_Wk1, L0_cond_bk1, L0_cond_Wk2, L0_cond_bk2, L0_cond_Wv, L0_cond_bv, L0_cond_alpha, L1_cond_Wx, L1_cond_Wh, L1_cond_b, L2_cond_Wx, L2_cond_Wh, L2_cond_b, L3_cond_Wx, L3_cond_Wh, L3_cond_b):
    import jax
    import jax.numpy as jnp

    def _L0_cond_ref(X1, X2, Wq1, bq1, Wq2, bq2, Wk1, bk1, Wk2, bk2, Wv, bv, alpha):
        import jax, jax.numpy as jnp
        import numpy as np
        D = 128
        B, S, Dm = X2.shape
        X1e = jnp.broadcast_to(X1[:, None, :], (B, S, Dm))
        X = jnp.concatenate([X1e, X2], axis=-1)
        Q1 = X1e @ Wq1 + bq1
        K1 = X1e @ Wk1 + bk1
        Q2 = X2 @ Wq2 + bq2
        K2 = X2 @ Wk2 + bk2
        V = X @ Wv + bv
        s = 1.0 / jnp.sqrt(jnp.float32(Dm))
        A1 = jnp.einsum('bqd,bkd->bqk', Q1, K1) * s
        A2 = jnp.einsum('bqd,bkd->bqk', Q2, K2) * s
        A = jax.nn.softmax(A2, axis=-1) - alpha * jax.nn.softmax(A1, axis=-1)
        return jnp.einsum('bqk,bkd->bqd', A, V)

    def _L1_cond_ref(x, h0, Wx, Wh, b):
        import jax, jax.numpy as jnp
        import numpy as np
        N, T, D, H = (64, 64, 128, 128)

        def lstm_scan(x, h0, Wx, Wh, b):
            xW = jnp.einsum('ntd,dg->ntg', x, Wx) + b
            Hdim = h0.shape[1]
            c0 = jnp.zeros_like(h0)

            def step(carry, xw_t):
                prev_h, prev_c = carry
                a = xw_t + prev_h @ Wh
                i = jax.nn.sigmoid(a[:, :Hdim])
                f = jax.nn.sigmoid(a[:, Hdim:2 * Hdim])
                o = jax.nn.sigmoid(a[:, 2 * Hdim:3 * Hdim])
                g = jnp.tanh(a[:, 3 * Hdim:])
                next_c = f * prev_c + i * g
                next_h = o * jnp.tanh(next_c)
                return ((next_h, next_c), next_h)
            _, hs = jax.lax.scan(step, (h0, c0), jnp.swapaxes(xW, 0, 1))
            return jnp.swapaxes(hs, 0, 1)
        return lstm_scan(x, h0, Wx, Wh, b)

    def _L2_cond_ref(x, h0, Wx, Wh, b):
        import jax, jax.numpy as jnp
        import numpy as np
        N, T, D, H = (128, 64, 128, 128)
        xW = jnp.einsum('ntd,dh->tnh', x, Wx) + b

        def step(h, xw_t):
            h_next = jnp.tanh(h @ Wh + xw_t)
            return (h_next, h_next)
        _, hs = jax.lax.scan(step, h0, xW)
        return jnp.swapaxes(hs, 0, 1)

    def _L3_cond_ref(x, h0, Wx, Wh, b):
        import jax, jax.numpy as jnp
        import numpy as np
        H = h0.shape[1]
        xW = jnp.einsum('ntd,dg->tng', x, Wx) + b

        def step(carry, xw_t):
            prev_h, prev_c = carry
            preact = xw_t + prev_h @ Wh
            i, f, o, g = jnp.split(preact, 4, axis=1)
            i = jax.nn.sigmoid(i)
            f = jax.nn.sigmoid(f)
            o = jax.nn.sigmoid(o)
            g = jnp.tanh(g)
            next_c = f * prev_c + i * g
            next_h = o * jnp.tanh(next_c)
            return ((next_h, next_c), next_h)
        c0 = jnp.zeros_like(h0)
        _, hs = jax.lax.scan(step, (h0, c0), xW)
        return jnp.transpose(hs, (1, 0, 2))
    x = x + _L0_cond_ref(cond_1024, x, L0_cond_Wq1, L0_cond_bq1, L0_cond_Wq2, L0_cond_bq2, L0_cond_Wk1, L0_cond_bk1, L0_cond_Wk2, L0_cond_bk2, L0_cond_Wv, L0_cond_bv, L0_cond_alpha)
    x = x + _L1_cond_ref(x, cond_1024, L1_cond_Wx, L1_cond_Wh, L1_cond_b)
    x = x + _L2_cond_ref(x, cond_1024, L2_cond_Wx, L2_cond_Wh, L2_cond_b)
    x = x + _L3_cond_ref(x, cond_1024, L3_cond_Wx, L3_cond_Wh, L3_cond_b)
    return x

_drawn_inputs = setup_inputs


def setup_inputs(seed=0):
    import zlib

    import numpy as np

    out = dict(_drawn_inputs(seed))
    spreads = {'L1_cond_b': (0.0, 0.1), 'L2_cond_b': (0.0, 0.1), 'L3_cond_b': (0.0, 0.34)}
    factors = {'L0_cond_bq2': 26.99, 'L0_cond_bk2': 64.0, 'L0_cond_bv': 8.0}
    for name, (base, spread) in spreads.items():
        noise = np.random.default_rng([zlib.crc32(name.encode()), seed]).standard_normal(out[name].shape)
        drawn = base * np.exp(spread * noise) if base else spread * noise
        out[name] = jnp.asarray(drawn.astype(out[name].dtype))
    for name, factor in factors.items():
        out[name] = (out[name] * factor).astype(out[name].dtype)
    return out
```

```python
import concourse.bass as bass
from concourse import mybir
from contextlib import ExitStack


def attention_then_stacked_recurrences(nc, x, cond, Wq1, bq1, Wq2, bq2, Wk1, bk1, Wk2, bk2, Wv, bv, alpha,
                                       L1_Wx, L1_Wh, L1_b, L2_Wx, L2_Wh, L2_b, L3_Wx, L3_Wh, L3_b, out):
    f32, bf16, f16, i32 = mybir.dt.float32, mybir.dt.bfloat16, mybir.dt.float16, mybir.dt.int32
    ALU = mybir.AluOpType
    ACT = mybir.ActivationFunctionType
    AX = mybir.AxisListType
    RMAX = bass.bass_isa.ReduceOp.max

    B, S, D = x.shape
    P = 128
    GB = P // S
    NG = B // GB
    NC = 4
    CG = NG // NC
    CT = CG * P
    CB = CG * GB
    NGATE = 4
    NP = S // 2
    PB = 2 * B
    SCALE = float(D) ** -0.5
    NW = 2 * NGATE + 1
    W1, W3, W2 = 0, NGATE, 2 * NGATE
    TOP = 12

    ctx = ExitStack()
    with ctx:
        def sb(name, shape, dt=f32):
            return ctx.enter_context(nc.sbuf_tensor(name, shape, dt))

        def sem(name):
            return ctx.enter_context(nc.semaphore(name))

        x_tok = sb("x_tok", [P, NG, D])
        xT = sb("xT", [D, B * S])
        qT = sb("qT", [D, B * S])
        kT = sb("kT", [D, B * S])
        v_tok = sb("v_tok", [P, NG, D])
        wq2, wk2 = sb("wq2", [D, D]), sb("wk2", [D, D])
        wq1, wk1 = sb("wq1", [D, D]), sb("wk1", [D, D])
        wv = sb("wv", [D, 2, D])
        cond_sb, condT = sb("cond_sb", [B, D]), sb("condT", [D, B])
        bias_rows, bias_cols = sb("bias_rows", [5, D]), sb("bias_cols", [D, 5])
        bv_row, alpha_sb = sb("bv_row", [1, D]), sb("alpha_sb", [P, 1])
        ident = sb("ident", [P, P])
        ones = sb("ones", [P, P])
        group_rows = sb("group_rows", [3 * GB, P], bf16)
        gate_cols = sb("gate_cols", [96, NGATE, PB], bf16)
        q1T, k1T, qk1 = sb("q1T", [D, B]), sb("k1T", [D, B]), sb("qk1", [D, B])
        s1, m1, d1 = sb("s1", [P, NG]), sb("m1", [P, NG]), sb("d1", [P, NG])
        e1, l1, p1 = sb("e1", [P, NG]), sb("l1", [P, NG]), sb("p1", [P, NG])
        v1_r1, v1_r2 = sb("v1_r1", [B, D]), sb("v1_r2", [B, D])
        v1_parts = sb("v1_parts", [B, 3, D], bf16)
        v1_rows = sb("v1_rows", [3 * GB, NG, D], bf16)
        sc_d, sc_e, prob = sb("sc_d", [P, NG, S]), sb("sc_e", [P, NG, S]), sb("prob", [P, NG, S])
        sc_m, sc_l = sb("sc_m", [P, NG]), sb("sc_l", [P, NG])
        probT = sb("probT", [P, NG, P])
        x1T = sb("x1T", [D, S, B])
        x2T = sb("x2T", [D, 2, 2, B])
        x3T = sb("x3T", [D, 2, 2, B])
        x4T = sb("x4T", [D, 2, 2, B])
        out_tok = sb("out_tok", [P, 2, D])
        WX, WXs = sb("WX", [D, NW, D]), sb("WXs", [D, NW, D])
        WH, WHs = sb("WH", [D, NW, D]), sb("WHs", [D, NW, D])
        WHhi, WHlo = sb("WHhi", [D, NW, D], f16), sb("WHlo", [D, NW, D], f16)
        amax, amax_all = sb("amax", [P, 1]), sb("amax_all", [P, 1])
        expo, up, down = sb("expo", [P, 1], i32), sb("up", [P, 1], i32), sb("down", [P, 1], i32)
        upf = sb("upf", [P, 1], i32)
        gb_in, gb_s = sb("gb_in", [96, 2, D]), sb("gb_s", [96, 2, D])
        gb_r1, gb_r2 = sb("gb_r1", [96, 2, D]), sb("gb_r2", [96, 2, D])
        gb_p = sb("gb_p", [96, 3, 2, D], bf16)
        gate_bias = sb("gate_bias", [96, 2, D], bf16)

        class Lstm:
            def __init__(self, n, w0, bias, bank0, lag):
                self.w0, self.bias, self.lag = w0, bias, lag
                self.banks = (bank0, bank0 + 1)
                self.gates = sb(f"gates{n}", [D, NGATE, B])
                self.fc, self.ig = sb(f"fc{n}", [D, B]), sb(f"ig{n}", [D, B])
                self.c, self.tc = sb(f"c{n}", [D, B]), sb(f"tc{n}", [D, B])
                self.h = sb(f"h{n}", [D, 2, B])
                self.hhi, self.hlo = sb(f"hhi{n}", [D, B], f16), sb(f"hlo{n}", [D, B], f16)
                self.x_ready = sem(f"x_part{n}_ready")
                self.pre = sem(f"preact{n}_ready")
                self.if_r, self.g_r, self.o_r = sem(f"if{n}_ready"), sem(f"g{n}_ready"), sem(f"o{n}_ready")
                self.tc_r = sem(f"tanh_c{n}_ready")
                self.terms, self.c_r = sem(f"c_terms{n}_ready"), sem(f"c{n}_ready")
                self.hhi_r, self.h_r, self.hlo_r = sem(f"hhi{n}_ready"), sem(f"h{n}_ready"), sem(f"hlo{n}_ready")
                self.sum_r = sem(f"x_after{n}_ready")

        bank = [ctx.enter_context(nc.psum_tensor(f"bank{i}", [P, 512], f32)) for i in range(8)]
        L1, L3 = Lstm(1, W1, 0, 0, 0), Lstm(3, W3, 1, 2, 2)
        RNN_BANK, OUT_BANK = 4, 6
        h2 = sb("h2", [D, 2, B])
        h2hi, h2lo = sb("h2hi", [D, B], f16), sb("h2lo", [D, B], f16)

        B_T, B_Q, B_K, B_V, B_S, B_O, B_SIDE = 0, 1, 2, 3, 4, 6, 7
        SIDE_C, SIDE_Q, SIDE_K, SIDE_V, SIDE_S, SIDE_B = 0, B, 2 * B, 3 * B, 3 * B + D, 3 * B + D + NG

        ld_x = [sem(f"ld_x{c}") for c in range(NC)]
        ld_cond, ld_rows, ld_q2, ld_k2 = sem("ld_cond"), sem("ld_rows"), sem("ld_q2"), sem("ld_k2")
        ld_qk1, ld_wv, ld_alpha = sem("ld_qk1"), sem("ld_wv"), sem("ld_alpha")
        ld_wh, ld_wx, ld_gb = sem("ld_wh"), sem("ld_wx"), sem("ld_gb")
        v1_moved, stored = sem("v1_moved"), [sem("stored_even"), sem("stored_odd")]
        zeroed, ident_ready, consts_ready = sem("zeroed"), sem("ident_ready"), sem("consts_ready")
        ones_ready, probT_zero = sem("ones_ready"), sem("probT_zero")
        xT_ps, xT_ready = sem("xT_in_psum"), sem("xT_ready")
        side_T, side_T_out = sem("side_transposed"), sem("side_copied")
        side_mm, qk1_ready, s1_ps, s1_ready = sem("side_products"), sem("qk1_ready"), sem("s1_in_psum"), sem("s1_ready")
        side_chain, p1_exp, p1_ready = sem("side_chain"), sem("p1_exp"), sem("p1_ready")
        v1_chain, v1_split = sem("v1_chain"), sem("v1_split")
        q_ps, k_ps, q_ready, k_ready = sem("q_in_psum"), sem("k_in_psum"), sem("q_ready"), sem("k_ready")
        v_ps, v_ready = sem("v_in_psum"), sem("v_ready")
        s_ps, sm_chain, sm_d, sm_e = sem("scores_in_psum"), sem("softmax_chain"), sem("scores_less_max"), sem("exp_ready")
        pT_ready, o_ps, x1_ready = sem("probT_ready"), sem("attn_in_psum"), sem("x1_ready")
        abs_ready = sem("abs_ready")
        amax_ready, amax_all_ready, scale_chain, scale_ready = (sem("amax_ready"), sem("amax_all_ready"),
                                                                sem("scale_chain"), sem("scale_ready"))
        ws_ready, wxs_ready, whi_ready, wlo_ready = (sem("WHs_ready"), sem("WXs_ready"), sem("WHhi_ready"),
                                                     sem("WHlo_ready"))
        gb_chain, gb_ready, state_zero = sem("gate_bias_chain"), sem("gate_bias_ready"), sem("cell_state_zeroed")
        x2_used, pre2, h2hi_r, h2_r, h2lo_r, sum2_r = (sem("x2_used"), sem("preact2_ready"), sem("hhi2_ready"),
                                                       sem("h2_ready"), sem("hlo2_ready"), sem("x_after2_ready"))
        out_ps, out_ready = sem("out_in_psum"), sem("out_ready")

        block = ctx.enter_context(nc.Block())

        x_v = x.rearrange("(g j) t d -> (j t) g d", j=GB)

        @block.sync
        def _(sp):
            for c in range(NC):
                sp.dma_start(x_tok[:, c * CG:(c + 1) * CG, :], x_v[:, c * CG:(c + 1) * CG, :]).then_inc(ld_x[c], 16)
                if c == 0:
                    sp.dma_start(wq2[:, :], Wq2).then_inc(ld_q2, 16)
                    sp.dma_start(wk2[:, :], Wk2).then_inc(ld_k2, 16)
            sp.wait_ge(v1_split, 1)
            for part in range(3):
                for j in range(GB):
                    r = part * GB + j
                    sp.dma_start(v1_rows[r:r + 1, :, :], v1_parts[j::GB, part, :]).then_inc(v1_moved, 16)
            for w, l in ((L1_Wh, W1), (L3_Wh, W3), (L2_Wh, W2)):
                n = w.shape[1] // D
                sp.dma_start(WH[:, l:l + n, :], w.rearrange("k (g n) -> k g n", n=D)).then_inc(ld_wh, 16)
            for w, l in ((L1_Wx, W1), (L2_Wx, W2), (L3_Wx, W3)):
                n = w.shape[1] // D
                sp.dma_start(WX[:, l:l + n, :], w.rearrange("k (g n) -> k g n", n=D)).then_inc(ld_wx, 16)
            for p in range(NP):
                sp.wait_ge(out_ready, p + 1)
                for s in range(2):
                    sp.dma_start(out[:, 2 * p + s, :], out_tok[s * B:(s + 1) * B, p % 2, :]).then_inc(stored[p % 2], 16)
            sp.wait_ge(stored[0], 16 * NP)
            sp.wait_ge(stored[1], 16 * NP)

        @block.gpsimd
        def _(pool):
            nc.gpsimd.memset(ident[:, :], 0.0).then_inc(zeroed, 1)
            nc.gpsimd.memset(ones[:, :], 1.0).then_inc(ones_ready, 1)
            nc.gpsimd.memset(group_rows[:, :], 0.0).then_inc(zeroed, 1)
            nc.gpsimd.memset(gate_cols[:, :, :], 0.0).then_inc(zeroed, 1)
            pool.wait_ge(zeroed, 1)
            nc.gpsimd.affine_select(out=ident[:, :], in_=ident[:, :], compare_op=ALU.not_equal, fill=1.0, base=0,
                                    pattern=[[-1, P]], channel_multiplier=1).then_inc(ident_ready, 1)
            pool.wait_ge(zeroed, 3)
            for part in range(3):
                if part:
                    pool.wait_ge(consts_ready, 2 * part)
                nc.gpsimd.affine_select(out=group_rows[:, :], in_=group_rows[:, :], compare_op=ALU.not_equal,
                                        fill=1.0, base=-GB * part, pattern=[[-1, GB], [0, S]],
                                        channel_multiplier=1).then_inc(consts_ready, 1)
                nc.gpsimd.affine_select(out=gate_cols[:, :, :], in_=gate_cols[:, :, :], compare_op=ALU.not_equal,
                                        fill=1.0, base=-32 * part, pattern=[[-1, NGATE], [0, PB]],
                                        channel_multiplier=1).then_inc(consts_ready, 1)
            nc.gpsimd.memset(probT[:, :, :], 0.0).then_inc(probT_zero, 1)
            pool.wait_ge(amax_ready, 1)
            nc.gpsimd.partition_all_reduce(amax_all[:, :], amax[:, :], P, RMAX).then_inc(amax_all_ready, 1)
            for n, (lo, hi) in enumerate(((W1, W3), (W2, NW), (W3, W2))):
                pool.wait_ge(ws_ready, n + 1)
                nc.gpsimd.tensor_copy(WHhi[:, lo:hi, :], WHs[:, lo:hi, :]).then_inc(whi_ready, 1)
                pool.wait_ge(whi_ready, n + 1)
                nc.gpsimd.tensor_tensor(WHlo[:, lo:hi, :], WHs[:, lo:hi, :], WHhi[:, lo:hi, :],
                                        ALU.subtract).then_inc(wlo_ready, 1)

            def sum1(t):
                p, s = t // 2, t % 2
                pool.wait_ge(L1.h_r, t + 1)
                if p >= 2 and s == 0:
                    pool.wait_ge(x2_used, p - 1)
                if p >= 2:
                    pool.wait_ge(sum2_r, 2 * p - 3 + s)
                nc.gpsimd.tensor_tensor(x2T[:, p % 2, s, :], x1T[:, t, :], L1.h[:, t % 2, :],
                                        ALU.add).then_inc(L1.sum_r, 1)

            def sum2(t):
                p, s = t // 2, t % 2
                pool.wait_ge(h2_r, t + 1)
                pool.wait_ge(L1.sum_r, t + 1)
                if p >= 2 and s == 0:
                    pool.wait_ge(L3.x_ready, p - 1)
                if p >= 2:
                    pool.wait_ge(L3.sum_r, 2 * p - 3 + s)
                nc.gpsimd.tensor_tensor(x3T[:, p % 2, s, :], x2T[:, p % 2, s, :], h2[:, t % 2, :],
                                        ALU.add).then_inc(sum2_r, 1)

            def sum3(t):
                p, s = t // 2, t % 2
                pool.wait_ge(L3.h_r, t + 1)
                pool.wait_ge(sum2_r, t + 1)
                if p >= 2 and s == 0:
                    pool.wait_ge(out_ps, p - 1)
                nc.gpsimd.tensor_tensor(x4T[:, p % 2, s, :], x3T[:, p % 2, s, :], L3.h[:, t % 2, :],
                                        ALU.add).then_inc(L3.sum_r, 1)

            for k in range(NP + 2):
                for s in range(2):
                    if s == 0 and 1 <= k <= NP:
                        sum2(2 * (k - 1))
                    if k < NP:
                        sum1(2 * k + s)
                    if s == 0 and 1 <= k <= NP:
                        sum2(2 * (k - 1) + 1)
                    if k >= 2:
                        sum3(2 * (k - 2) + s)

        @block.scalar
        def _(act):
            act.dma_start(cond_sb[:, :], cond).then_inc(ld_cond, 16)
            for r, b in enumerate((bq1, bk1, bq2, bk2, L2_b)):
                act.dma_start(bias_rows[r:r + 1, :], b.unsqueeze(0)).then_inc(ld_rows, 16)
            act.dma_start(bv_row[:, :], bv.unsqueeze(0)).then_inc(ld_rows, 16)
            act.dma_start(wv[:, :, :], Wv.rearrange("(h k) n -> k h n", h=2)).then_inc(ld_wv, 16)
            act.dma_start(wq1[:, :], Wq1).then_inc(ld_qk1, 16)
            act.dma_start(wk1[:, :], Wk1).then_inc(ld_qk1, 16)
            act.dma_start(alpha_sb[:, :], alpha.partition_broadcast(P)).then_inc(ld_alpha, 16)
            act.wait_ge(state_zero, 3)
            for part in range(3):
                for n, b in enumerate((L1_b, L3_b)):
                    act.dma_start(gb_in[32 * part:32 * part + NGATE, n, :],
                                  b.rearrange("(g n) -> g n", n=D)).then_inc(ld_gb, 16)

            def exp_of(c):
                g = slice(c * CG, (c + 1) * CG)
                act.wait_ge(sm_d, c + 1)
                nc.scalar.activation(sc_e[:, g, :], sc_d[:, g, :], ACT.Exp, scale=SCALE).then_inc(sm_e, 1)

            for c in range(NC):
                cols = slice(c * CT, (c + 1) * CT)
                if c == 0:
                    act.wait_ge(side_T_out, 2)
                act.wait_ge(q_ps, c + 1)
                nc.scalar.activation(qT[:, cols], bank[B_Q][:, :], ACT.Identity,
                                     bias=bias_cols[:, 2:3]).then_inc(q_ready, 1)
                act.wait_ge(k_ps, c + 1)
                nc.scalar.activation(kT[:, cols], bank[B_K][:, :], ACT.Identity,
                                     bias=bias_cols[:, 3:4]).then_inc(k_ready, 1)
                exp_of(c)
                act.wait_ge(v_ps, c + 1)
                nc.scalar.activation(v_tok[:, c * CG:(c + 1) * CG, :],
                                     bank[B_V][:, :].rearrange("p (g d) -> p g d", d=D),
                                     ACT.Copy).then_inc(v_ready, 1)
                if c == 0:
                    act.wait_ge(p1_exp, 1)
                    nc.scalar.activation(e1[:, :], d1[:, :], ACT.Exp, scale=SCALE).then_inc(p1_exp, 1)
                if c == 1:
                    act.wait_ge(ld_wh, 48)
                    nc.scalar.activation(WHs[:, :, :], WH[:, :, :], ACT.Abs).then_inc(abs_ready, 1)
                if c == 2:
                    act.wait_ge(scale_ready, 1)
                    act.wait_ge(ld_wx, 48)
                    for lo, hi in ((W1, W3), (W2, NW), (W3, W2)):
                        nc.scalar.activation(WHs[:, lo:hi, :], WH[:, lo:hi, :], ACT.Copy,
                                             scale=upf[:, 0:1].bitcast(f32)).then_inc(ws_ready, 1)
                    for lo, hi in ((W1, W3), (W2, NW), (W3, W2)):
                        nc.scalar.activation(WXs[:, lo:hi, :], WX[:, lo:hi, :], ACT.Copy,
                                             scale=upf[:, 0:1].bitcast(f32)).then_inc(wxs_ready, 1)
            unscale = act.alloc_register("unscale")
            act.reg_load(unscale, down[0:1, 0:1])

            def pair_cols(bk, g0, g1, s):
                return bank[bk][:, :].rearrange("p (g s b) -> p g s b", g=NGATE, s=2)[:, g0:g1, s, :]

            def gate_functions(L, t):
                bk, s = L.banks[(t // 2) % 2], t % 2
                act.wait_ge(L.pre, t + 1)
                if t:
                    act.wait_ge(L.c_r, t)
                nc.scalar.activation(L.gates[:, 0:2, :], pair_cols(bk, 0, 2, s), ACT.Sigmoid,
                                     scale=unscale).then_inc(L.if_r, 1)
                nc.scalar.activation(L.gates[:, 3:4, :], pair_cols(bk, 3, 4, s), ACT.Tanh,
                                     scale=unscale).then_inc(L.g_r, 1)
                if t:
                    act.wait_ge(L.h_r, t)
                nc.scalar.activation(L.gates[:, 2:3, :], pair_cols(bk, 2, 3, s), ACT.Sigmoid,
                                     scale=unscale).then_inc(L.o_r, 1)

            def tanh_c(L, t):
                act.wait_ge(L.c_r, t + 1)
                nc.scalar.activation(L.tc[:, :], L.c[:, :], ACT.Tanh).then_inc(L.tc_r, 1)

            def rnn(t):
                act.wait_ge(pre2, t + 1)
                z = bank[RNN_BANK + (t // 2) % 2][:, (t % 2) * B:(t % 2 + 1) * B]
                if t >= 2:
                    act.wait_ge(sum2_r, t - 1)
                nc.scalar.activation(h2[:, t % 2, :], z, ACT.Tanh, bias=bias_cols[:, 4:5],
                                     scale=unscale).then_inc(h2_r, 1)

            for k in range(NP + 3):
                for s in range(2):
                    if k < NP:
                        gate_functions(L1, 2 * k + s)
                    if s == 0 and 1 <= k <= NP:
                        rnn(2 * (k - 1))
                    if k < NP:
                        tanh_c(L1, 2 * k + s)
                    if s == 0 and k >= 3:
                        p = k - 3
                        act.wait_ge(out_ps, p + 1)
                        if p >= 2:
                            act.wait_ge(stored[p % 2], 32 * (p // 2))
                        nc.scalar.activation(out_tok[:, p % 2, :], bank[OUT_BANK + p % 2][:, 0:D],
                                             ACT.Copy).then_inc(out_ready, 1)
                    if 2 <= k < NP + 2:
                        gate_functions(L3, 2 * (k - 2) + s)
                    if s == 0 and 1 <= k <= NP:
                        rnn(2 * (k - 1) + 1)
                    if 2 <= k < NP + 2:
                        tanh_c(L3, 2 * (k - 2) + s)

        @block.vector
        def _(dve):
            for L in (L1, L3):
                nc.vector.memset(L.c[:, :], 0.0).then_inc(state_zero, 1)
            nc.vector.memset(gb_in[:, :, :], 0.0).then_inc(state_zero, 1)

            def copy_xT(c):
                dve.wait_ge(xT_ps, c + 1)
                nc.vector.tensor_copy(xT[:, c * CT:(c + 1) * CT], bank[B_T][:, :]).then_inc(xT_ready, 1)

            def softmax(c):
                g = slice(c * CG, (c + 1) * CG)
                n = 5 * c
                sc = bank[B_S + c % 2][:, 0:CG * S].rearrange("p (g k) -> p g k", k=S)
                dve.wait_ge(s_ps, c + 1)
                nc.vector.tensor_reduce(sc_m[:, g], sc, axis=AX.X, op=ALU.max).then_inc(sm_chain, 1)
                dve.wait_ge(sm_chain, n + 1)
                nc.vector.tensor_tensor(sc_d[:, g, :], sc, sc_m[:, g].unsqueeze(2).to_broadcast([P, CG, S]),
                                        ALU.subtract).then_inc(sm_d, 1)
                dve.wait_ge(sm_e, c + 1)
                nc.vector.tensor_reduce(sc_l[:, g], sc_e[:, g, :], axis=AX.X, op=ALU.add).then_inc(sm_chain, 1)
                dve.wait_ge(sm_chain, n + 2)
                nc.vector.reciprocal(sc_m[:, g], sc_l[:, g]).then_inc(sm_chain, 1)
                dve.wait_ge(sm_chain, n + 3)
                nc.vector.tensor_tensor(sc_d[:, g, :], sc_e[:, g, :],
                                        sc_m[:, g].unsqueeze(2).to_broadcast([P, CG, S]),
                                        ALU.mult).then_inc(sm_chain, 1)
                dve.wait_ge(sm_chain, n + 4)
                if c == 0:
                    first_softmax_end()
                nc.vector.tensor_tensor(prob[:, g, :], sc_d[:, g, :],
                                        p1[:, g].unsqueeze(2).to_broadcast([P, CG, S]),
                                        ALU.subtract).then_inc(sm_chain, 1)
                dve.wait_ge(sm_chain, n + 5)
                if c == 0:
                    dve.wait_ge(probT_zero, 1)
                for j in range(GB):
                    q = slice(j * S, (j + 1) * S)
                    nc.vector.transpose(probT[q, g, q], prob[q, g, :]).then_inc(pT_ready, 1)

            def residual(c):
                dve.wait_ge(o_ps, c + 1)
                nc.vector.tensor_tensor(x1T[:, :, c * CB:(c + 1) * CB].rearrange("p t b -> p b t"),
                                        bank[B_O][:, :].rearrange("p (b t) -> p b t", t=S),
                                        xT[:, c * CT:(c + 1) * CT].rearrange("p (b t) -> p b t", t=S),
                                        ALU.add).then_inc(x1_ready, 1)

            def first_softmax_start():
                dve.wait_ge(s1_ps, 1)
                nc.vector.tensor_copy(s1[:, :], bank[B_SIDE][:, SIDE_S:SIDE_S + NG]).then_inc(side_chain, 1)
                dve.wait_ge(side_chain, 1)
                nc.vector.tensor_reduce(m1[:, :], s1[:, :].unsqueeze(2).to_broadcast([P, NG, S]), axis=AX.X,
                                        op=ALU.max).then_inc(side_chain, 1)
                dve.wait_ge(side_chain, 2)
                nc.vector.tensor_tensor(d1[:, :], s1[:, :], m1[:, :], ALU.subtract).then_inc(p1_exp, 1)

            def first_softmax_end():
                dve.wait_ge(p1_exp, 2)
                nc.vector.tensor_reduce(l1[:, :], e1[:, :].unsqueeze(2).to_broadcast([P, NG, S]), axis=AX.X,
                                        op=ALU.add).then_inc(side_chain, 1)
                dve.wait_ge(side_chain, 3)
                nc.vector.reciprocal(m1[:, :], l1[:, :]).then_inc(side_chain, 1)
                dve.wait_ge(side_chain, 4)
                dve.wait_ge(ld_alpha, 16)
                nc.vector.scalar_tensor_tensor(out=p1[:, :], in0=m1[:, :], scalar=alpha_sb[:, 0:1], in1=e1[:, :],
                                               op0=ALU.mult, op1=ALU.mult).then_inc(side_chain, 1)
                dve.wait_ge(side_chain, 5)

            dve.wait_ge(side_T, 2)
            nc.vector.tensor_copy(condT[:, :], bank[B_SIDE][:, SIDE_C:SIDE_C + B]).then_inc(side_T_out, 1)
            nc.vector.tensor_copy(bias_cols[:, :], bank[B_SIDE][:, SIDE_B:SIDE_B + 5]).then_inc(side_T_out, 1)
            copy_xT(0)
            dve.wait_ge(side_mm, 1)
            v1_ps = bank[B_SIDE][0:B, SIDE_V:SIDE_V + D]
            nc.vector.tensor_copy(v1_parts[:, 0, :], v1_ps).then_inc(v1_chain, 1)
            dve.wait_ge(v1_chain, 1)
            nc.vector.tensor_tensor(v1_r1[:, :], v1_ps, v1_parts[:, 0, :], ALU.subtract).then_inc(v1_chain, 1)
            dve.wait_ge(v1_chain, 2)
            nc.vector.tensor_copy(v1_parts[:, 1, :], v1_r1[:, :]).then_inc(v1_chain, 1)
            dve.wait_ge(v1_chain, 3)
            nc.vector.tensor_tensor(v1_r2[:, :], v1_r1[:, :], v1_parts[:, 1, :], ALU.subtract).then_inc(v1_chain, 1)
            dve.wait_ge(v1_chain, 4)
            nc.vector.tensor_copy(v1_parts[:, 2, :], v1_r2[:, :]).then_inc(v1_split, 1)
            copy_xT(1)
            dve.wait_ge(side_mm, 2)
            dve.wait_ge(side_T_out, 2)
            nc.vector.tensor_scalar(q1T[:, :], bank[B_SIDE][:, SIDE_Q:SIDE_Q + B], bias_cols[:, 0:1], None,
                                    ALU.add).then_inc(qk1_ready, 1)
            nc.vector.tensor_scalar(k1T[:, :], bank[B_SIDE][:, SIDE_K:SIDE_K + B], bias_cols[:, 1:2], None,
                                    ALU.add).then_inc(qk1_ready, 1)
            dve.wait_ge(qk1_ready, 2)
            nc.vector.tensor_tensor(qk1[:, :], q1T[:, :], k1T[:, :], ALU.mult).then_inc(qk1_ready, 1)
            first_softmax_start()
            softmax(0)
            copy_xT(2)
            softmax(1)
            residual(0)
            dve.wait_ge(abs_ready, 1)
            nc.vector.tensor_reduce(amax[:, :], WHs[:, :, :], axis=AX.XY, op=ALU.max).then_inc(amax_ready, 1)
            copy_xT(3)
            dve.wait_ge(amax_all_ready, 1)
            nc.vector.tensor_scalar(expo[:, :], amax_all[:, :].bitcast(i32), 23, None,
                                    ALU.logical_shift_right).then_inc(scale_chain, 1)
            dve.wait_ge(scale_chain, 1)
            nc.vector.tensor_scalar(up[:, :], expo[:, :], -1, 254 + TOP, ALU.mult, ALU.add).then_inc(scale_chain, 1)
            dve.wait_ge(scale_chain, 2)
            nc.vector.tensor_scalar(up[:, :], up[:, :], 127 + 2 * TOP, None, ALU.min).then_inc(scale_chain, 1)
            dve.wait_ge(scale_chain, 3)
            nc.vector.tensor_scalar(expo[:, :], up[:, :], -1, 254, ALU.mult, ALU.add).then_inc(scale_chain, 1)
            nc.vector.tensor_scalar(upf[:, :], up[:, :], 23, None, ALU.logical_shift_left).then_inc(scale_chain, 1)
            dve.wait_ge(scale_chain, 5)
            nc.vector.tensor_scalar(down[:, :], expo[:, :], 23, None, ALU.logical_shift_left).then_inc(scale_ready, 1)
            softmax(2)
            residual(1)
            dve.wait_ge(ld_gb, 96)
            nc.vector.tensor_scalar(gb_s[:, :, :], gb_in[:, :, :], upf[0:96, 0:1].bitcast(f32), None,
                                    ALU.mult).then_inc(gb_chain, 1)
            dve.wait_ge(gb_chain, 1)
            nc.vector.tensor_copy(gb_p[:, 0, :, :], gb_s[:, :, :]).then_inc(gb_chain, 1)
            dve.wait_ge(gb_chain, 2)
            nc.vector.tensor_tensor(gb_r1[:, :, :], gb_s[:, :, :], gb_p[:, 0, :, :], ALU.subtract).then_inc(gb_chain, 1)
            dve.wait_ge(gb_chain, 3)
            nc.vector.tensor_copy(gb_p[:, 1, :, :], gb_r1[:, :, :]).then_inc(gb_chain, 1)
            dve.wait_ge(gb_chain, 4)
            nc.vector.tensor_tensor(gb_r2[:, :, :], gb_r1[:, :, :], gb_p[:, 1, :, :], ALU.subtract).then_inc(gb_chain, 1)
            dve.wait_ge(gb_chain, 5)
            nc.vector.tensor_copy(gb_p[:, 2, :, :], gb_r2[:, :, :]).then_inc(gb_chain, 1)
            dve.wait_ge(gb_chain, 6)
            for part in range(3):
                q = slice(32 * part, 32 * part + 32)
                nc.vector.tensor_copy(gate_bias[q, :, :], gb_p[q, part, :, :]).then_inc(gb_ready, 1)
            softmax(3)
            residual(2)
            residual(3)

            def cell(L, t):
                dve.wait_ge(L.if_r, t + 1)
                if t:
                    dve.wait_ge(L.c_r, t)
                else:
                    dve.wait_ge(state_zero, 3)
                nc.vector.tensor_tensor(L.fc[:, :], L.gates[:, 1, :], L.c[:, :], ALU.mult).then_inc(L.terms, 1)
                dve.wait_ge(L.g_r, t + 1)
                nc.vector.tensor_tensor(L.ig[:, :], L.gates[:, 0, :], L.gates[:, 3, :], ALU.mult).then_inc(L.terms, 1)
                dve.wait_ge(L.terms, 2 * t + 2)
                if t:
                    dve.wait_ge(L.tc_r, t)
                nc.vector.tensor_tensor(L.c[:, :], L.fc[:, :], L.ig[:, :], ALU.add).then_inc(L.c_r, 1)

            def hidden(L, t):
                dve.wait_ge(L.tc_r, t + 1)
                dve.wait_ge(L.o_r, t + 1)
                nc.vector.tensor_tensor(L.hhi[:, :], L.gates[:, 2, :], L.tc[:, :], ALU.mult).then_inc(L.hhi_r, 1)
                if t >= 2:
                    dve.wait_ge(L.sum_r, t - 1)
                nc.vector.tensor_tensor(L.h[:, t % 2, :], L.gates[:, 2, :], L.tc[:, :], ALU.mult).then_inc(L.h_r, 1)
                dve.wait_ge(L.h_r, t + 1)
                nc.vector.tensor_tensor(L.hlo[:, :], L.h[:, t % 2, :], L.hhi[:, :], ALU.subtract).then_inc(L.hlo_r, 1)

            def rnn_split(t):
                dve.wait_ge(h2_r, t + 1)
                nc.vector.tensor_copy(h2hi[:, :], h2[:, t % 2, :]).then_inc(h2hi_r, 1)
                dve.wait_ge(h2hi_r, t + 1)
                nc.vector.tensor_tensor(h2lo[:, :], h2[:, t % 2, :], h2hi[:, :], ALU.subtract).then_inc(h2lo_r, 1)

            for k in range(NP + 2):
                for s in range(2):
                    if k < NP:
                        cell(L1, 2 * k + s)
                    if s == 0 and 1 <= k <= NP:
                        rnn_split(2 * (k - 1))
                    if k < NP:
                        hidden(L1, 2 * k + s)
                    if k >= 2:
                        cell(L3, 2 * (k - 2) + s)
                    if s == 0 and 1 <= k <= NP:
                        rnn_split(2 * (k - 1) + 1)
                    if k >= 2:
                        hidden(L3, 2 * (k - 2) + s)

        @block.tensor
        def _(pe):
            mm = nc.tensor.matmul

            def transpose_x(c):
                if c == 0:
                    pe.wait_ge(ident_ready, 1)
                else:
                    pe.wait_ge(xT_ready, c)
                pe.wait_ge(ld_x[c], 16)
                for g in range(CG):
                    last = nc.tensor.transpose(bank[B_T][:, g * P:(g + 1) * P], x_tok[:, c * CG + g, :], ident[:, :])
                last.then_inc(xT_ps, 1)

            def project_qk(c):
                cols = slice(c * CT, (c + 1) * CT)
                pe.wait_ge(xT_ready, c + 1)
                if c:
                    pe.wait_ge(q_ready, c)
                    pe.wait_ge(k_ready, c)
                else:
                    pe.wait_ge(ld_q2, 16)
                mm(bank[B_Q][:, :], wq2[:, :], xT[:, cols], start=True, stop=True).then_inc(q_ps, 1)
                if c == 0:
                    pe.wait_ge(ld_k2, 16)
                mm(bank[B_K][:, :], wk2[:, :], xT[:, cols], start=True, stop=True).then_inc(k_ps, 1)

            def project_v(c):
                if c:
                    pe.wait_ge(v_ready, c)
                else:
                    pe.wait_ge(consts_ready, 6)
                    pe.wait_ge(v1_moved, 16 * 3 * GB)
                mm(bank[B_V][:, :], group_rows[:, :],
                   v1_rows[:, c * CG:(c + 1) * CG, :].rearrange("r g d -> r (g d)"),
                   start=True, stop=False, skip_group_check=True)
                for g in range(CG):
                    last = mm(bank[B_V][:, g * D:(g + 1) * D], xT[:, c * CT + g * P:c * CT + (g + 1) * P], wv[:, 1, :],
                              start=False, stop=True, skip_group_check=True)
                last.then_inc(v_ps, 1)

            def scores(c):
                pe.wait_ge(q_ready, c + 1)
                pe.wait_ge(k_ready, c + 1)
                if c >= 2:
                    pe.wait_ge(sm_d, c - 1)
                for g in range(CG):
                    for j in range(GB):
                        tok = slice((c * CB + g * GB + j) * S, (c * CB + g * GB + j + 1) * S)
                        last = mm(bank[B_S + c % 2][j * S:(j + 1) * S, g * S:(g + 1) * S], qT[:, tok], kT[:, tok],
                                  start=True, stop=True)
                last.then_inc(s_ps, 1)

            def attend(c):
                pe.wait_ge(pT_ready, GB * (c + 1))
                pe.wait_ge(v_ready, c + 1)
                if c:
                    pe.wait_ge(x1_ready, c)
                for g in range(CG):
                    last = mm(bank[B_O][:, g * P:(g + 1) * P], v_tok[:, c * CG + g, :], probT[:, c * CG + g, :],
                              start=True, stop=True)
                last.then_inc(o_ps, 1)

            def side_transposes():
                pe.wait_ge(ident_ready, 1)
                pe.wait_ge(ld_cond, 16)
                nc.tensor.transpose(bank[B_SIDE][:, SIDE_C:SIDE_C + B], cond_sb[:, :],
                                    ident[0:B, 0:B]).then_inc(side_T, 1)
                pe.wait_ge(ld_rows, 96)
                nc.tensor.transpose(bank[B_SIDE][:, SIDE_B:SIDE_B + 5], bias_rows[:, :],
                                    ident[0:5, 0:5]).then_inc(side_T, 1)

            def side_products():
                pe.wait_ge(side_T_out, 2)
                pe.wait_ge(ones_ready, 1)
                pe.wait_ge(ld_wv, 16)
                mm(bank[B_SIDE][0:B, SIDE_V:SIDE_V + D], condT[:, :], wv[:, 0, :], start=True, stop=False)
                mm(bank[B_SIDE][0:B, SIDE_V:SIDE_V + D], ones[0:1, 0:B], bv_row[:, :],
                   start=False, stop=True).then_inc(side_mm, 1)

            def side_products_qk1():
                pe.wait_ge(ld_qk1, 32)
                pe.wait_ge(v1_split, 1)
                mm(bank[B_SIDE][:, SIDE_Q:SIDE_Q + B], wq1[:, :], condT[:, :], start=True, stop=True)
                mm(bank[B_SIDE][:, SIDE_K:SIDE_K + B], wk1[:, :], condT[:, :], start=True,
                   stop=True).then_inc(side_mm, 1)

            def side_scores():
                pe.wait_ge(qk1_ready, 3)
                qk_v = qk1[:, :].rearrange("d (g j) -> d j g", j=GB)
                for j in range(GB):
                    last = mm(bank[B_SIDE][j * S:(j + 1) * S, SIDE_S:SIDE_S + NG], ones[:, 0:S], qk_v[:, j, :],
                              start=True, stop=True)
                last.then_inc(s1_ps, 1)

            side_transposes()
            transpose_x(0)
            side_products()
            project_qk(0)
            transpose_x(1)
            side_products_qk1()
            scores(0)
            side_scores()
            project_v(0)
            project_qk(1)
            transpose_x(2)
            scores(1)
            project_v(1)
            attend(0)
            project_qk(2)
            transpose_x(3)
            scores(2)
            project_v(2)
            attend(1)
            project_qk(3)
            scores(3)
            project_v(3)
            attend(2)
            attend(3)

            def gates_from_x(L, xin, p, half):
                bk = bank[L.banks[p % 2]]
                if half == 0:
                    mm(bk[:, :], gate_bias[:, L.bias, :], gate_cols[:, :, :].rearrange("r g n -> r (g n)"),
                       start=True, stop=False, skip_group_check=True)
                for g in (0, 1) if half == 0 else (2, 3):
                    last = mm(bk[:, g * PB:(g + 1) * PB], WXs[:, L.w0 + g, :], xin,
                              start=False, stop=False, skip_group_check=True)
                if half:
                    last.then_inc(L.x_ready, 1)

            def split_product(ps, w, hhi, hlo, hhi_r, hlo_r, t, gates):
                pe.wait_ge(hhi_r, t)
                for g in gates:
                    for part in (WHhi, WHlo):
                        mm(ps(g), part[:, w + g, :], hhi[:, :], start=False, stop=False, skip_group_check=True)
                pe.wait_ge(hlo_r, t)
                for g in gates:
                    for part in (WHhi, WHlo):
                        last = mm(ps(g), part[:, w + g, :], hlo[:, :], start=False, stop=part is WHlo,
                                  skip_group_check=True)
                return last

            def first_product(ps, w, gates):
                for g in gates:
                    last = mm(ps(g), WHs[:, w + g, :], condT[:, :], start=False, stop=True, skip_group_check=True)
                return last

            def lstm_step(L, t):
                bk, s = bank[L.banks[(t // 2) % 2]], t % 2
                ps = lambda g: bk[:, g * PB + s * B:g * PB + (s + 1) * B]
                gates = (1, 0, 3, 2)
                if t == 0:
                    last = first_product(ps, L.w0, gates)
                else:
                    last = split_product(ps, L.w0, L.hhi, L.hlo, L.hhi_r, L.hlo_r, t, gates)
                last.then_inc(L.pre, 1)

            def rnn_x(p):
                pe.wait_ge(L1.sum_r, 2 * p + 2)
                mm(bank[RNN_BANK + p % 2][:, 0:PB], WXs[:, W2, :], x2T[:, p % 2, :, :].rearrange("d s b -> d (s b)"),
                   start=True, stop=False, skip_group_check=True).then_inc(x2_used, 1)

            def rnn_step(t):
                bk, s = bank[RNN_BANK + (t // 2) % 2], t % 2
                ps = lambda g: bk[:, s * B:(s + 1) * B]
                if t == 0:
                    last = first_product(ps, W2, (0,))
                else:
                    last = split_product(ps, W2, h2hi, h2lo, h2hi_r, h2lo_r, t, (0,))
                last.then_inc(pre2, 1)

            def x_of(xin, p):
                return xin[:, p % 2, :, :].rearrange("d s b -> d (s b)")

            def x1_of(p):
                return x1T[:, 2 * p:2 * p + 2, :].rearrange("d s b -> d (s b)")

            pe.wait_ge(x1_ready, NC)
            pe.wait_ge(wxs_ready, 3)
            pe.wait_ge(gb_ready, 3)
            gates_from_x(L1, x1_of(0), 0, 0)
            gates_from_x(L1, x1_of(0), 0, 1)
            for k in range(NP + 3):
                if k < NP:
                    lstm_step(L1, 2 * k)
                if k == 0:
                    pe.wait_ge(wlo_ready, 3)
                if 1 <= k <= NP:
                    rnn_x(k - 1)
                    rnn_step(2 * (k - 1))
                if k + 1 < NP:
                    gates_from_x(L1, x1_of(k + 1), k + 1, 0)
                if 2 <= k < NP + 2:
                    lstm_step(L3, 2 * (k - 2))
                if k + 1 < NP:
                    gates_from_x(L1, x1_of(k + 1), k + 1, 1)
                if 1 <= k <= NP:
                    rnn_step(2 * (k - 1) + 1)
                if k >= 3:
                    p = k - 3
                    pe.wait_ge(L3.sum_r, 2 * p + 2)
                    if p >= 2:
                        pe.wait_ge(out_ready, p - 1)
                    nc.tensor.transpose(bank[OUT_BANK + p % 2][:, 0:D], x_of(x4T, p),
                                        ident[:, :]).then_inc(out_ps, 1)
                if k < NP:
                    lstm_step(L1, 2 * k + 1)
                if 1 <= k <= NP:
                    pe.wait_ge(sum2_r, 2 * (k - 1) + 2)
                    gates_from_x(L3, x_of(x3T, k - 1), k - 1, 0)
                if 2 <= k < NP + 2:
                    lstm_step(L3, 2 * (k - 2) + 1)
                if 1 <= k <= NP:
                    gates_from_x(L3, x_of(x3T, k - 1), k - 1, 1)


_INS = ['x', 'cond_1024', 'L0_cond_Wq1', 'L0_cond_bq1', 'L0_cond_Wq2', 'L0_cond_bq2', 'L0_cond_Wk1', 'L0_cond_bk1',
        'L0_cond_Wk2', 'L0_cond_bk2', 'L0_cond_Wv', 'L0_cond_bv', 'L0_cond_alpha', 'L1_cond_Wx', 'L1_cond_Wh',
        'L1_cond_b', 'L2_cond_Wx', 'L2_cond_Wh', 'L2_cond_b', 'L3_cond_Wx', 'L3_cond_Wh', 'L3_cond_b']


def kernel(**inputs):
    import numpy as np
    import concourse.bacc as bacc
    from concourse.bass_utils import run_bass_kernel_spmd

    nc = bacc.Bacc("TRN2", target_bir_lowering=False, num_devices=1)
    arrays, args = {}, []
    for name in _INS:
        a = np.ascontiguousarray(inputs[name])
        if a.ndim == 0:
            a = a.reshape(1)
        arrays[f"in_{name}"] = a
        args.append(nc.dram_tensor(f"in_{name}", a.shape, mybir.dt.from_np(a.dtype), kind="ExternalInput").ap())
    shape = tuple(inputs['x'].shape)
    args.append(nc.dram_tensor("out", shape, mybir.dt.float32, kind="ExternalOutput").ap())
    attention_then_stacked_recurrences(nc, *args)
    r = run_bass_kernel_spmd(nc, [arrays], core_ids=[0])
    return r.results[0]["out"]
```

```python
import concourse.bass as bass
from concourse import mybir
from contextlib import ExitStack


def attention_then_stacked_recurrences(nc, xT_in, small_in, wqk_in, wv_in, gate_bias_in, wh_in, wx_in, out):
    f32, bf16, f16, i32 = mybir.dt.float32, mybir.dt.bfloat16, mybir.dt.float16, mybir.dt.int32
    ALU = mybir.AluOpType
    ACT = mybir.ActivationFunctionType
    AX = mybir.AxisListType
    RMAX = bass.bass_isa.ReduceOp.max

    D, B, S = xT_in.shape
    P = 128
    GB = P // S
    NG = B // GB
    NC = 4
    CG = NG // NC
    CT = CG * P
    CB = CG * GB
    NGATE = 4
    NP = S // 2
    PB = 2 * B
    SCALE = float(D) ** -0.5
    NW = 2 * NGATE + 1
    W1, W3, W2 = 0, NGATE, 2 * NGATE
    WARM = 8
    TOP = 12

    ctx = ExitStack()
    with ctx:
        def sb(name, shape, dt=f32):
            return ctx.enter_context(nc.sbuf_tensor(name, shape, dt))

        def sem(name):
            return ctx.enter_context(nc.semaphore(name))

        xT = sb("xT", [D, B * S])
        qT = sb("qT", [D, B * S])
        kT = sb("kT", [D, B * S])
        v_tok = sb("v_tok", [P, NG, D])
        small = sb("small", [P, 2 * B + 6 + D])
        condT = small[:, 0:B]
        condT_jg = small[:, B:2 * B]
        BQ1, BK1, BQ2, BK2, B2, ALPHA = (small[:, 2 * B + i:2 * B + i + 1] for i in range(6))
        bv_row = small[0:1, 2 * B + 6:2 * B + 6 + D]
        wqk = sb("wqk", [D, 2, D])
        wv = sb("wv", [D, 4, D])
        ones = sb("ones", [P, P])
        warm = sb("warm", [P, 512], bf16)
        group_rows = sb("group_rows", [3 * GB, P], bf16)
        gate_cols = sb("gate_cols", [96, NGATE, PB], bf16)
        q1T, k1T, qk1 = sb("q1T", [D, B]), sb("k1T", [D, B]), sb("qk1", [D, B])
        s1, m1, d1 = sb("s1", [P, NG]), sb("m1", [P, NG]), sb("d1", [P, NG])
        e1, l1, p1 = sb("e1", [P, NG]), sb("l1", [P, NG]), sb("p1", [P, NG])
        v1_r1, v1_r2 = sb("v1_r1", [B, D]), sb("v1_r2", [B, D])
        v1_parts = sb("v1_parts", [B, 3, D], bf16)
        v1_rows = sb("v1_rows", [3 * GB, NG, D], bf16)
        sc_d, sc_e, prob = sb("sc_d", [P, NG, S]), sb("sc_e", [P, NG, S]), sb("prob", [P, NG, S])
        sc_m, sc_l = sb("sc_m", [P, NG]), sb("sc_l", [P, NG])
        probT = sb("probT", [P, NG, P])
        x_run = sb("x_run", [D, S, B])
        WX, WXs = sb("WX", [D, NW, D]), sb("WXs", [D, NW, D])
        WH, WHs = sb("WH", [D, NW, D]), sb("WHs", [D, NW, D])
        WHhi, WHlo = sb("WHhi", [D, NW, D], f16), sb("WHlo", [D, NW, D], f16)
        amax, amax_all = sb("amax", [P, 1]), sb("amax_all", [P, 1])
        expo, up, down = sb("expo", [P, 1], i32), sb("up", [P, 1], i32), sb("down", [P, 1], i32)
        upf = sb("upf", [P, 1], i32)
        gb_in, gb_s = sb("gb_in", [96, 2, D]), sb("gb_s", [96, 2, D])
        gb_r1, gb_r2 = sb("gb_r1", [96, 2, D]), sb("gb_r2", [96, 2, D])
        gb_p = sb("gb_p", [96, 3, 2, D], bf16)
        gate_bias = sb("gate_bias", [96, 2, D], bf16)

        class Lstm:
            def __init__(self, n, w0, bias, bank0, lag):
                self.w0, self.bias, self.lag = w0, bias, lag
                self.banks = (bank0, bank0 + 1)
                self.gates = sb(f"gates{n}", [D, NGATE, B])
                self.fc, self.ig = sb(f"fc{n}", [D, B]), sb(f"ig{n}", [D, B])
                self.c, self.tc = sb(f"c{n}", [D, B]), sb(f"tc{n}", [D, B])
                self.h = sb(f"h{n}", [D, 2, B])
                self.hhi, self.hlo = sb(f"hhi{n}", [D, B], f16), sb(f"hlo{n}", [D, B], f16)
                self.pre = sem(f"preact{n}_ready")
                self.if_r, self.g_r, self.o_r = sem(f"if{n}_ready"), sem(f"g{n}_ready"), sem(f"o{n}_ready")
                self.tc_r = sem(f"tanh_c{n}_ready")
                self.fc_r, self.ig_r, self.c_r = sem(f"fc{n}_ready"), sem(f"ig{n}_ready"), sem(f"c{n}_ready")
                self.hhi_r, self.h_r, self.hlo_r = sem(f"hhi{n}_ready"), sem(f"h{n}_ready"), sem(f"hlo{n}_ready")
                self.sum_r = sem(f"x_after{n}_ready")

        bank = [ctx.enter_context(nc.psum_tensor(f"bank{i}", [P, 512], f32)) for i in range(8)]
        L1, L3 = Lstm(1, W1, 0, 0, 0), Lstm(3, W3, 1, 2, 2)
        RNN_BANK = 4
        h2 = sb("h2", [D, 2, B])
        h2hi, h2lo = sb("h2hi", [D, B], f16), sb("h2lo", [D, B], f16)

        B_Q, B_K, B_V, B_S, B_O, B_SIDE = 1, 2, 3, 4, 6, 7
        SIDE_Q, SIDE_K, SIDE_V, SIDE_S = B, 2 * B, 3 * B, 3 * B + D

        ld_x = [sem(f"ld_x{c}") for c in range(NC)]
        ld_small, ld_qk, ld_wv = sem("ld_small"), sem("ld_qk_weights"), sem("ld_v_weights")
        ld_wh, ld_wx, ld_gb = sem("ld_wh"), sem("ld_wx"), sem("ld_gate_bias")
        v1_moved, stored, warm_zero = sem("v1_moved"), sem("stored"), sem("warm_zeroed")
        zeroed, rows_ready, cols_ready = sem("zeroed"), sem("group_rows_ready"), sem("gate_cols_ready")
        ones_ready, probT_zero = sem("ones_ready"), sem("probT_zero")
        side_mm, qk1_ready, s1_ps, s1_ready = sem("side_products"), sem("qk1_ready"), sem("s1_in_psum"), sem("s1_ready")
        side_chain, p1_exp, p1_ready = sem("side_chain"), sem("p1_exp"), sem("p1_ready")
        v1_chain, v1_split = sem("v1_chain"), sem("v1_split")
        q_ps, k_ps, q_ready, k_ready = sem("q_in_psum"), sem("k_in_psum"), sem("q_ready"), sem("k_ready")
        v_ps, v_ready = sem("v_in_psum"), sem("v_ready")
        s_ps, sm_chain, sm_d, sm_e = sem("scores_in_psum"), sem("softmax_chain"), sem("scores_less_max"), sem("exp_ready")
        pT_ready, o_ps, x1_ready = sem("probT_ready"), sem("attn_in_psum"), sem("x1_ready")
        abs_ready = sem("abs_ready")
        amax_ready, amax_all_ready, scale_chain, scale_ready = (sem("amax_ready"), sem("amax_all_ready"),
                                                                sem("scale_chain"), sem("scale_ready"))
        ws_ready, wxs_ready, whi_ready, wlo_ready = (sem("WHs_ready"), sem("WXs_ready"), sem("WHhi_ready"),
                                                     sem("WHlo_ready"))
        gb_chain, gb_ready, state_zero = sem("gate_bias_chain"), sem("gate_bias_ready"), sem("cell_state_zeroed")
        pre2, h2hi_r, h2_r, h2lo_r, sum2_r = (sem("preact2_ready"), sem("hhi2_ready"),
                                                       sem("h2_ready"), sem("hlo2_ready"), sem("x_after2_ready"))

        block = ctx.enter_context(nc.Block())

        @block.sync
        def _(sp):
            x_v = xT_in.rearrange("d b t -> d (b t)")
            sp.dma_start(wqk[:, :, :], wqk_in).then_inc(ld_qk, 16)
            for c in range(NC):
                cols = slice(c * CT, (c + 1) * CT)
                sp.dma_start(xT[:, cols], x_v[:, cols]).then_inc(ld_x[c], 16)
            sp.dma_start(WH[:, :, :], wh_in).then_inc(ld_wh, 16)
            sp.dma_start(WX[:, :, :], wx_in).then_inc(ld_wx, 16)
            sp.dma_start(gb_in[:, :, :], gate_bias_in).then_inc(ld_gb, 16)
            sp.wait_ge(v1_split, 1)
            for part in range(3):
                sp.dma_start(v1_rows[part * GB:(part + 1) * GB, :, :], v1_parts[:, part, :]).then_inc(v1_moved, 16)
            for p in range(NP):
                sp.wait_ge(L3.sum_r, 2 * p + 2)
                sp.dma_start(out[:, 2 * p:2 * p + 2, :], x_run[:, 2 * p:2 * p + 2, :]).then_inc(stored, 16)
            sp.wait_ge(stored, 16 * NP)

        @block.gpsimd
        def _(pool):
            nc.gpsimd.memset(ones[:, :], 1.0).then_inc(ones_ready, 1)
            nc.gpsimd.memset(group_rows[:, :], 0.0).then_inc(zeroed, 1)
            nc.gpsimd.memset(gate_cols[:, :, :], 0.0).then_inc(zeroed, 1)
            for part in range(3):
                pool.wait_ge(zeroed, 1) if part == 0 else pool.wait_ge(rows_ready, part)
                nc.gpsimd.affine_select(out=group_rows[:, :], in_=group_rows[:, :], compare_op=ALU.not_equal,
                                        fill=1.0, base=-GB * part, pattern=[[-1, GB], [0, S]],
                                        channel_multiplier=1).then_inc(rows_ready, 1)
            nc.gpsimd.memset(probT[:, :, :], 0.0).then_inc(probT_zero, 1)
            for part in range(3):
                pool.wait_ge(zeroed, 2) if part == 0 else pool.wait_ge(cols_ready, part)
                nc.gpsimd.affine_select(out=gate_cols[:, :, :], in_=gate_cols[:, :, :], compare_op=ALU.not_equal,
                                        fill=1.0, base=-32 * part, pattern=[[-1, NGATE], [0, PB]],
                                        channel_multiplier=1).then_inc(cols_ready, 1)
            pool.wait_ge(amax_ready, 1)
            nc.gpsimd.partition_all_reduce(amax_all[:, :], amax[:, :], P, RMAX).then_inc(amax_all_ready, 1)
            for n, (lo, hi) in enumerate(((W1, W3), (W2, NW), (W3, W2))):
                pool.wait_ge(ws_ready, n + 1)
                nc.gpsimd.tensor_copy(WHhi[:, lo:hi, :], WHs[:, lo:hi, :]).then_inc(whi_ready, 1)
                pool.wait_ge(whi_ready, n + 1)
                nc.gpsimd.tensor_tensor(WHlo[:, lo:hi, :], WHs[:, lo:hi, :], WHhi[:, lo:hi, :],
                                        ALU.subtract).then_inc(wlo_ready, 1)

            def sum1(t):
                pool.wait_ge(L1.h_r, t + 1)
                nc.gpsimd.tensor_tensor(x_run[:, t, :], x_run[:, t, :], L1.h[:, t % 2, :],
                                        ALU.add).then_inc(L1.sum_r, 1)

            def sum2(t):
                pool.wait_ge(h2_r, t + 1)
                pool.wait_ge(L1.sum_r, t + 1)
                nc.gpsimd.tensor_tensor(x_run[:, t, :], x_run[:, t, :], h2[:, t % 2, :],
                                        ALU.add).then_inc(sum2_r, 1)

            def sum3(t):
                pool.wait_ge(L3.h_r, t + 1)
                pool.wait_ge(sum2_r, t + 1)
                nc.gpsimd.tensor_tensor(x_run[:, t, :], x_run[:, t, :], L3.h[:, t % 2, :],
                                        ALU.add).then_inc(L3.sum_r, 1)

            def kept_cell(L, t):
                pool.wait_ge(L.if_r, t + 1)
                if t:
                    pool.wait_ge(L.c_r, t)
                else:
                    pool.wait_ge(state_zero, 2)
                nc.gpsimd.tensor_tensor(L.fc[:, :], L.gates[:, 1, :], L.c[:, :], ALU.mult).then_inc(L.fc_r, 1)

            for t in range(S + 5):
                if t < S:
                    kept_cell(L1, t)
                if t >= 5:
                    sum3(t - 5)
                if 2 <= t < S + 2 and t % 2 == 0:
                    sum2(t - 2)
                if 4 <= t < S + 4:
                    kept_cell(L3, t - 4)
                if t < S:
                    sum1(t)
                if 2 <= t < S + 2 and t % 2 == 0:
                    sum2(t - 1)

        @block.scalar
        def _(act):
            act.dma_start(small[:, :], small_in).then_inc(ld_small, 16)
            act.dma_start(wv[:, :, :], wv_in).then_inc(ld_wv, 16)

            def exp_of(c):
                g = slice(c * CG, (c + 1) * CG)
                act.wait_ge(sm_d, c + 1)
                nc.scalar.activation(sc_e[:, g, :], sc_d[:, g, :], ACT.Exp, scale=SCALE).then_inc(sm_e, 1)

            for c in range(NC):
                cols = slice(c * CT, (c + 1) * CT)
                if c == 0:
                    act.wait_ge(ld_small, 16)
                act.wait_ge(q_ps, c + 1)
                nc.scalar.activation(qT[:, cols], bank[B_Q][:, :], ACT.Identity,
                                     bias=BQ2).then_inc(q_ready, 1)
                act.wait_ge(k_ps, c + 1)
                nc.scalar.activation(kT[:, cols], bank[B_K][:, :], ACT.Identity,
                                     bias=BK2).then_inc(k_ready, 1)
                exp_of(c)
                act.wait_ge(v_ps, c + 1)
                nc.scalar.activation(v_tok[:, c * CG:(c + 1) * CG, :],
                                     bank[B_V][:, :].rearrange("p (g d) -> p g d", d=D),
                                     ACT.Copy).then_inc(v_ready, 1)
                if c == 0:
                    act.wait_ge(p1_exp, 1)
                    nc.scalar.activation(e1[:, :], d1[:, :], ACT.Exp, scale=SCALE).then_inc(p1_exp, 1)
                if c == 0:
                    act.wait_ge(ld_wh, 16)
                    nc.scalar.activation(WHs[:, :, :], WH[:, :, :], ACT.Abs).then_inc(abs_ready, 1)
                if c == 1:
                    act.wait_ge(scale_ready, 1)
                    act.wait_ge(ld_wx, 16)
                    for lo, hi in ((W1, W3), (W2, NW), (W3, W2)):
                        nc.scalar.activation(WHs[:, lo:hi, :], WH[:, lo:hi, :], ACT.Copy,
                                             scale=upf[:, 0:1].bitcast(f32)).then_inc(ws_ready, 1)
                    for lo, hi in ((W1, W3), (W2, NW), (W3, W2)):
                        nc.scalar.activation(WXs[:, lo:hi, :], WX[:, lo:hi, :], ACT.Copy,
                                             scale=upf[:, 0:1].bitcast(f32)).then_inc(wxs_ready, 1)
            unscale = act.alloc_register("unscale")
            act.reg_load(unscale, down[0:1, 0:1])

            def pair_cols(bk, g0, g1, s):
                return bank[bk][:, :].rearrange("p (g s b) -> p g s b", g=NGATE, s=2)[:, g0:g1, s, :]

            def gate_functions(L, t):
                bk, s = L.banks[(t // 2) % 2], t % 2
                act.wait_ge(L.pre, t + 1)
                if t:
                    act.wait_ge(L.c_r, t)
                nc.scalar.activation(L.gates[:, 0:2, :], pair_cols(bk, 0, 2, s), ACT.Sigmoid,
                                     scale=unscale).then_inc(L.if_r, 1)
                nc.scalar.activation(L.gates[:, 3:4, :], pair_cols(bk, 3, 4, s), ACT.Tanh,
                                     scale=unscale).then_inc(L.g_r, 1)
                if t:
                    act.wait_ge(L.h_r, t)
                nc.scalar.activation(L.gates[:, 2:3, :], pair_cols(bk, 2, 3, s), ACT.Sigmoid,
                                     scale=unscale).then_inc(L.o_r, 1)

            def tanh_c(L, t):
                act.wait_ge(L.c_r, t + 1)
                nc.scalar.activation(L.tc[:, :], L.c[:, :], ACT.Tanh).then_inc(L.tc_r, 1)

            def rnn(t):
                act.wait_ge(pre2, t + 1)
                z = bank[RNN_BANK + (t // 2) % 2][:, (t % 2) * B:(t % 2 + 1) * B]
                if t >= 2:
                    act.wait_ge(sum2_r, t - 1)
                nc.scalar.activation(h2[:, t % 2, :], z, ACT.Tanh, bias=B2,
                                     scale=unscale).then_inc(h2_r, 1)
                if t:
                    act.wait_ge(h2lo_r, t)
                nc.scalar.activation(h2hi[:, :], z, ACT.Tanh, bias=B2,
                                     scale=unscale).then_inc(h2hi_r, 1)

            for t in range(S + 4):
                if t < S:
                    gate_functions(L1, t)
                if 2 <= t < S + 2 and t % 2 == 0:
                    rnn(t - 2)
                if t < S:
                    tanh_c(L1, t)
                if 4 <= t < S + 4:
                    gate_functions(L3, t - 4)
                if 2 <= t < S + 2 and t % 2 == 0:
                    rnn(t - 1)
                if 4 <= t < S + 4:
                    tanh_c(L3, t - 4)

        @block.vector
        def _(dve):
            nc.vector.memset(warm[:, :], 0.0).then_inc(warm_zero, 1)
            for L in (L1, L3):
                nc.vector.memset(L.c[:, :], 0.0).then_inc(state_zero, 1)

            def softmax(c):
                g = slice(c * CG, (c + 1) * CG)
                n = 5 * c
                sc = bank[B_S + c % 2][:, 0:CG * S].rearrange("p (g k) -> p g k", k=S)
                dve.wait_ge(s_ps, c + 1)
                nc.vector.tensor_reduce(sc_m[:, g], sc, axis=AX.X, op=ALU.max).then_inc(sm_chain, 1)
                dve.wait_ge(sm_chain, n + 1)
                nc.vector.tensor_tensor(sc_d[:, g, :], sc, sc_m[:, g].unsqueeze(2).to_broadcast([P, CG, S]),
                                        ALU.subtract).then_inc(sm_d, 1)
                dve.wait_ge(sm_e, c + 1)
                nc.vector.tensor_reduce(sc_l[:, g], sc_e[:, g, :], axis=AX.X, op=ALU.add).then_inc(sm_chain, 1)
                dve.wait_ge(sm_chain, n + 2)
                nc.vector.reciprocal(sc_m[:, g], sc_l[:, g]).then_inc(sm_chain, 1)
                dve.wait_ge(sm_chain, n + 3)
                nc.vector.tensor_tensor(sc_d[:, g, :], sc_e[:, g, :],
                                        sc_m[:, g].unsqueeze(2).to_broadcast([P, CG, S]),
                                        ALU.mult).then_inc(sm_chain, 1)
                dve.wait_ge(sm_chain, n + 4)
                if c == 0:
                    first_softmax_end()
                nc.vector.tensor_tensor(prob[:, g, :], sc_d[:, g, :],
                                        p1[:, g].unsqueeze(2).to_broadcast([P, CG, S]),
                                        ALU.subtract).then_inc(sm_chain, 1)
                dve.wait_ge(sm_chain, n + 5)
                if c == 0:
                    dve.wait_ge(probT_zero, 1)
                for j in range(GB):
                    q = slice(j * S, (j + 1) * S)
                    nc.vector.transpose(probT[q, g, q], prob[q, g, :]).then_inc(pT_ready, 1)

            def residual(c):
                dve.wait_ge(o_ps, c + 1)
                nc.vector.tensor_tensor(x_run[:, :, c * CB:(c + 1) * CB].rearrange("p t b -> p b t"),
                                        bank[B_O][:, :].rearrange("p (b t) -> p b t", t=S),
                                        xT[:, c * CT:(c + 1) * CT].rearrange("p (b t) -> p b t", t=S),
                                        ALU.add).then_inc(x1_ready, 1)

            def first_softmax_start():
                dve.wait_ge(s1_ps, 1)
                nc.vector.tensor_copy(s1[:, :], bank[B_SIDE][:, SIDE_S:SIDE_S + NG]).then_inc(side_chain, 1)
                dve.wait_ge(side_chain, 1)
                nc.vector.tensor_reduce(m1[:, :], s1[:, :].unsqueeze(2).to_broadcast([P, NG, S]), axis=AX.X,
                                        op=ALU.max).then_inc(side_chain, 1)
                dve.wait_ge(side_chain, 2)
                nc.vector.tensor_tensor(d1[:, :], s1[:, :], m1[:, :], ALU.subtract).then_inc(p1_exp, 1)

            def first_softmax_end():
                dve.wait_ge(p1_exp, 2)
                nc.vector.tensor_reduce(l1[:, :], e1[:, :].unsqueeze(2).to_broadcast([P, NG, S]), axis=AX.X,
                                        op=ALU.add).then_inc(side_chain, 1)
                dve.wait_ge(side_chain, 3)
                nc.vector.reciprocal(m1[:, :], l1[:, :]).then_inc(side_chain, 1)
                dve.wait_ge(side_chain, 4)
                nc.vector.scalar_tensor_tensor(out=p1[:, :], in0=m1[:, :], scalar=ALPHA, in1=e1[:, :],
                                               op0=ALU.mult, op1=ALU.mult).then_inc(side_chain, 1)
                dve.wait_ge(side_chain, 5)

            dve.wait_ge(side_mm, 1)
            v1_ps = bank[B_SIDE][0:B, SIDE_V:SIDE_V + D]
            nc.vector.tensor_copy(v1_parts[:, 0, :], v1_ps).then_inc(v1_chain, 1)
            dve.wait_ge(v1_chain, 1)
            nc.vector.tensor_tensor(v1_r1[:, :], v1_ps, v1_parts[:, 0, :], ALU.subtract).then_inc(v1_chain, 1)
            dve.wait_ge(v1_chain, 2)
            nc.vector.tensor_copy(v1_parts[:, 1, :], v1_r1[:, :]).then_inc(v1_chain, 1)
            dve.wait_ge(v1_chain, 3)
            nc.vector.tensor_tensor(v1_r2[:, :], v1_r1[:, :], v1_parts[:, 1, :], ALU.subtract).then_inc(v1_chain, 1)
            dve.wait_ge(v1_chain, 4)
            nc.vector.tensor_copy(v1_parts[:, 2, :], v1_r2[:, :]).then_inc(v1_split, 1)
            dve.wait_ge(side_mm, 2)
            dve.wait_ge(ld_small, 16)
            nc.vector.tensor_scalar(q1T[:, :], bank[B_SIDE][:, SIDE_Q:SIDE_Q + B], BQ1, None,
                                    ALU.add).then_inc(qk1_ready, 1)
            nc.vector.tensor_scalar(k1T[:, :], bank[B_SIDE][:, SIDE_K:SIDE_K + B], BK1, None,
                                    ALU.add).then_inc(qk1_ready, 1)
            dve.wait_ge(qk1_ready, 2)
            nc.vector.tensor_tensor(qk1[:, :], q1T[:, :], k1T[:, :], ALU.mult).then_inc(qk1_ready, 1)
            first_softmax_start()
            softmax(0)
            dve.wait_ge(abs_ready, 1)
            nc.vector.tensor_reduce(amax[:, :], WHs[:, :, :], axis=AX.XY, op=ALU.max).then_inc(amax_ready, 1)
            dve.wait_ge(amax_all_ready, 1)
            nc.vector.tensor_scalar(expo[:, :], amax_all[:, :].bitcast(i32), 23, None,
                                    ALU.logical_shift_right).then_inc(scale_chain, 1)
            dve.wait_ge(scale_chain, 1)
            nc.vector.tensor_scalar(up[:, :], expo[:, :], -1, 254 + TOP, ALU.mult, ALU.add).then_inc(scale_chain, 1)
            dve.wait_ge(scale_chain, 2)
            nc.vector.tensor_scalar(up[:, :], up[:, :], 127 + 2 * TOP, None, ALU.min).then_inc(scale_chain, 1)
            dve.wait_ge(scale_chain, 3)
            nc.vector.tensor_scalar(expo[:, :], up[:, :], -1, 254, ALU.mult, ALU.add).then_inc(scale_chain, 1)
            nc.vector.tensor_scalar(upf[:, :], up[:, :], 23, None, ALU.logical_shift_left).then_inc(scale_chain, 1)
            dve.wait_ge(scale_chain, 5)
            nc.vector.tensor_scalar(down[:, :], expo[:, :], 23, None, ALU.logical_shift_left).then_inc(scale_ready, 1)
            softmax(1)
            residual(0)
            dve.wait_ge(ld_gb, 16)
            nc.vector.tensor_scalar(gb_s[:, :, :], gb_in[:, :, :], upf[0:96, 0:1].bitcast(f32), None,
                                    ALU.mult).then_inc(gb_chain, 1)
            dve.wait_ge(gb_chain, 1)
            nc.vector.tensor_copy(gb_p[:, 0, :, :], gb_s[:, :, :]).then_inc(gb_chain, 1)
            dve.wait_ge(gb_chain, 2)
            nc.vector.tensor_tensor(gb_r1[:, :, :], gb_s[:, :, :], gb_p[:, 0, :, :], ALU.subtract).then_inc(gb_chain, 1)
            dve.wait_ge(gb_chain, 3)
            nc.vector.tensor_copy(gb_p[:, 1, :, :], gb_r1[:, :, :]).then_inc(gb_chain, 1)
            dve.wait_ge(gb_chain, 4)
            nc.vector.tensor_tensor(gb_r2[:, :, :], gb_r1[:, :, :], gb_p[:, 1, :, :], ALU.subtract).then_inc(gb_chain, 1)
            dve.wait_ge(gb_chain, 5)
            nc.vector.tensor_copy(gb_p[:, 2, :, :], gb_r2[:, :, :]).then_inc(gb_chain, 1)
            dve.wait_ge(gb_chain, 6)
            for part in range(3):
                q = slice(32 * part, 32 * part + 32)
                nc.vector.tensor_copy(gate_bias[q, :, :], gb_p[q, part, :, :]).then_inc(gb_ready, 1)
            softmax(2)
            residual(1)
            softmax(3)
            residual(2)
            residual(3)

            def new_cell_term(L, t):
                dve.wait_ge(L.g_r, t + 1)
                nc.vector.tensor_tensor(L.ig[:, :], L.gates[:, 0, :], L.gates[:, 3, :], ALU.mult).then_inc(L.ig_r, 1)

            def cell(L, t):
                dve.wait_ge(L.ig_r, t + 1)
                dve.wait_ge(L.fc_r, t + 1)
                if t:
                    dve.wait_ge(L.tc_r, t)
                nc.vector.tensor_tensor(L.c[:, :], L.fc[:, :], L.ig[:, :], ALU.add).then_inc(L.c_r, 1)

            def hidden(L, t):
                dve.wait_ge(L.tc_r, t + 1)
                dve.wait_ge(L.o_r, t + 1)
                nc.vector.tensor_tensor(L.hhi[:, :], L.gates[:, 2, :], L.tc[:, :], ALU.mult).then_inc(L.hhi_r, 1)
                if t >= 2:
                    dve.wait_ge(L.sum_r, t - 1)
                nc.vector.tensor_tensor(L.h[:, t % 2, :], L.gates[:, 2, :], L.tc[:, :], ALU.mult).then_inc(L.h_r, 1)

            def hidden_low(L, t):
                dve.wait_ge(L.h_r, t + 1)
                nc.vector.tensor_tensor(L.hlo[:, :], L.h[:, t % 2, :], L.hhi[:, :], ALU.subtract).then_inc(L.hlo_r, 1)

            def rnn_split(t):
                dve.wait_ge(h2_r, t + 1)
                dve.wait_ge(h2hi_r, t + 1)
                nc.vector.tensor_tensor(h2lo[:, :], h2[:, t % 2, :], h2hi[:, :], ALU.subtract).then_inc(h2lo_r, 1)

            for t in range(S + 4):
                in1, in3 = t < S, 4 <= t
                if in1:
                    new_cell_term(L1, t)
                if t >= 5:
                    hidden_low(L3, t - 5)
                if in1:
                    cell(L1, t)
                if 2 <= t < S + 2 and t % 2 == 0:
                    rnn_split(t - 2)
                if in1:
                    hidden(L1, t)
                if in3:
                    new_cell_term(L3, t - 4)
                if in1:
                    hidden_low(L1, t)
                if in3:
                    cell(L3, t - 4)
                if 2 <= t < S + 2 and t % 2 == 0:
                    rnn_split(t - 1)
                if in3:
                    hidden(L3, t - 4)

        @block.tensor
        def _(pe):
            mm = nc.tensor.matmul

            def project_qk(c):
                cols = slice(c * CT, (c + 1) * CT)
                pe.wait_ge(ld_x[c], 16)
                if c:
                    pe.wait_ge(q_ready, c)
                    pe.wait_ge(k_ready, c)
                else:
                    pe.wait_ge(ld_qk, 16)
                mm(bank[B_Q][:, :], wqk[:, 0, :], xT[:, cols], start=True, stop=True).then_inc(q_ps, 1)
                mm(bank[B_K][:, :], wqk[:, 1, :], xT[:, cols], start=True, stop=True).then_inc(k_ps, 1)

            def project_v(c):
                if c:
                    pe.wait_ge(v_ready, c)
                else:
                    pe.wait_ge(ld_wv, 16)
                for g in range(CG):
                    mm(bank[B_V][:, g * D:(g + 1) * D], xT[:, c * CT + g * P:c * CT + (g + 1) * P], wv[:, 1, :],
                       start=g == 0, stop=False, skip_group_check=True)
                if c == 0:
                    pe.wait_ge(rows_ready, 3)
                    pe.wait_ge(v1_moved, 16 * 3)
                mm(bank[B_V][:, :], group_rows[:, :],
                   v1_rows[:, c * CG:(c + 1) * CG, :].rearrange("r g d -> r (g d)"),
                   start=False, stop=True, skip_group_check=True).then_inc(v_ps, 1)

            def scores(c):
                pe.wait_ge(q_ready, c + 1)
                pe.wait_ge(k_ready, c + 1)
                if c >= 2:
                    pe.wait_ge(sm_d, c - 1)
                for g in range(CG):
                    for j in range(GB):
                        tok = slice((c * CB + g * GB + j) * S, (c * CB + g * GB + j + 1) * S)
                        last = mm(bank[B_S + c % 2][j * S:(j + 1) * S, g * S:(g + 1) * S], qT[:, tok], kT[:, tok],
                                  start=True, stop=True)
                last.then_inc(s_ps, 1)

            def attend(c):
                pe.wait_ge(pT_ready, GB * (c + 1))
                pe.wait_ge(v_ready, c + 1)
                if c:
                    pe.wait_ge(x1_ready, c)
                for g in range(CG):
                    last = mm(bank[B_O][:, g * P:(g + 1) * P], v_tok[:, c * CG + g, :], probT[:, c * CG + g, :],
                              start=True, stop=True)
                last.then_inc(o_ps, 1)

            def side_products():
                pe.wait_ge(ld_small, 16)
                pe.wait_ge(ones_ready, 1)
                pe.wait_ge(ld_wv, 16)
                mm(bank[B_SIDE][0:B, SIDE_V:SIDE_V + D], condT_jg, wv[:, 0, :], start=True, stop=False)
                mm(bank[B_SIDE][0:B, SIDE_V:SIDE_V + D], ones[0:1, 0:B], bv_row,
                   start=False, stop=True).then_inc(side_mm, 1)

            def side_products_qk1():
                pe.wait_ge(v1_split, 1)
                mm(bank[B_SIDE][:, SIDE_Q:SIDE_Q + B], wv[:, 2, :], condT_jg, start=True, stop=True)
                mm(bank[B_SIDE][:, SIDE_K:SIDE_K + B], wv[:, 3, :], condT_jg, start=True,
                   stop=True).then_inc(side_mm, 1)

            def side_scores():
                pe.wait_ge(qk1_ready, 3)
                for j in range(GB):
                    last = mm(bank[B_SIDE][j * S:(j + 1) * S, SIDE_S:SIDE_S + NG], ones[:, 0:S],
                              qk1[:, j * NG:(j + 1) * NG],
                              start=True, stop=True)
                last.then_inc(s1_ps, 1)

            pe.wait_ge(warm_zero, 1)
            for _ in range(WARM):
                mm(bank[0][:, :], warm[:, 0:P], warm[:, :], start=True, stop=True)
            side_products()
            project_qk(0)
            side_products_qk1()
            project_qk(1)
            scores(0)
            side_scores()
            project_v(0)
            project_qk(2)
            scores(1)
            attend(0)
            project_v(1)
            project_qk(3)
            scores(2)
            attend(1)
            project_v(2)
            scores(3)
            project_v(3)
            attend(2)
            attend(3)

            def bias_half(L, p, half):
                g = slice(2 * half, 2 * half + 2)
                mm(bank[L.banks[p % 2]][:, 2 * half * PB:(2 * half + 2) * PB], gate_bias[:, L.bias, :],
                   gate_cols[:, g, :].rearrange("r g n -> r (g n)"),
                   start=half == 0, stop=False, skip_group_check=True)

            def gates_from_x(L, p, gates):
                for g in gates:
                    mm(bank[L.banks[p % 2]][:, g * PB:(g + 1) * PB], WXs[:, L.w0 + g, :], x_of(p),
                       start=False, stop=False, skip_group_check=True)

            def split_product(ps, w, hhi, hlo, hhi_r, hlo_r, t, gates, between=None):
                pe.wait_ge(hhi_r, t)
                for g in gates:
                    for part in (WHhi, WHlo):
                        mm(ps(g), part[:, w + g, :], hhi[:, :], start=False, stop=False, skip_group_check=True)
                if between:
                    between()
                pe.wait_ge(hlo_r, t)
                for g in gates:
                    last = mm(ps(g), WHhi[:, w + g, :], hlo[:, :], start=False, stop=True, skip_group_check=True)
                return last

            def first_product(ps, w, gates):
                for g in gates:
                    last = mm(ps(g), WHs[:, w + g, :], condT, start=False, stop=True, skip_group_check=True)
                return last

            def lstm_step(L, t, between=None):
                bk, s = bank[L.banks[(t // 2) % 2]], t % 2
                ps = lambda g: bk[:, g * PB + s * B:g * PB + (s + 1) * B]
                gates = (1, 0, 3, 2)
                if t == 0:
                    last = first_product(ps, L.w0, gates)
                    if between:
                        between()
                else:
                    last = split_product(ps, L.w0, L.hhi, L.hlo, L.hhi_r, L.hlo_r, t, gates, between)
                last.then_inc(L.pre, 1)

            def x_of(p):
                return x_run[:, 2 * p:2 * p + 2, :].rearrange("d s b -> d (s b)")

            def rnn_x(p):
                pe.wait_ge(L1.sum_r, 2 * p + 2)
                mm(bank[RNN_BANK + p % 2][:, 0:PB], WXs[:, W2, :], x_of(p),
                   start=True, stop=False, skip_group_check=True)

            def rnn_step(t):
                bk, s = bank[RNN_BANK + (t // 2) % 2], t % 2
                ps = lambda g: bk[:, s * B:(s + 1) * B]
                if t == 0:
                    last = first_product(ps, W2, (0,))
                else:
                    last = split_product(ps, W2, h2hi, h2lo, h2hi_r, h2lo_r, t, (0,))
                last.then_inc(pre2, 1)

            pe.wait_ge(gb_ready, 3)
            pe.wait_ge(cols_ready, 3)
            bias_half(L1, 0, 0)
            bias_half(L1, 0, 1)
            pe.wait_ge(wxs_ready, 3)
            pe.wait_ge(x1_ready, NC)
            gates_from_x(L1, 0, (0, 1, 2, 3))
            for k in range(NP + 2):
                in1, next1, in2, in3 = k < NP, k + 1 < NP, 1 <= k <= NP, k >= 2
                if in1:
                    lstm_step(L1, 2 * k, (lambda: bias_half(L1, k + 1, 0)) if next1 else None)
                if k == 0:
                    pe.wait_ge(wlo_ready, 3)
                if in3:
                    gates_from_x(L3, k - 2, (2, 3))
                if in2:
                    rnn_x(k - 1)
                    rnn_step(2 * (k - 1))
                if in3:
                    lstm_step(L3, 2 * (k - 2), (lambda: bias_half(L1, k + 1, 1)) if next1 else None)
                elif next1:
                    bias_half(L1, k + 1, 1)
                if next1:
                    gates_from_x(L1, k + 1, (0, 1))
                if in2:
                    rnn_step(2 * (k - 1) + 1)
                if in1:
                    lstm_step(L1, 2 * k + 1, (lambda: bias_half(L3, k - 1, 0)) if in2 else None)
                elif in2:
                    bias_half(L3, k - 1, 0)
                if next1:
                    gates_from_x(L1, k + 1, (2, 3))
                if in3:
                    lstm_step(L3, 2 * (k - 2) + 1, (lambda: bias_half(L3, k - 1, 1)) if in2 else None)
                elif in2:
                    bias_half(L3, k - 1, 1)
                if in2:
                    pe.wait_ge(sum2_r, 2 * (k - 1) + 2)
                    gates_from_x(L3, k - 1, (0, 1))

def kernel(**inputs):
    import numpy as np
    import concourse.bacc as bacc
    from concourse.bass_utils import run_bass_kernel_spmd

    a = {name.replace("L0_cond_", "").replace("_cond_", "_"): np.asarray(v) for name, v in inputs.items()}
    cond = a["cond_1024"]
    B, D = cond.shape
    S = a["x"].shape[1]
    GB, NGATE = 128 // S, 4

    def column(v):
        return np.broadcast_to(v.reshape(-1, 1), (D, 1))

    def blocks(*ws):
        return np.concatenate([w.reshape(D, -1, D) for w in ws], axis=1)

    cond_jg = cond.reshape(B // GB, GB, D).transpose(1, 0, 2).reshape(B, D)
    bv = np.zeros((D, D), a["bv"].dtype)
    bv[0] = a["bv"]
    gate_bias = np.zeros((96, 2, D), a["L1_b"].dtype)
    for row in range(0, 96, 32):
        gate_bias[row:row + NGATE, 0] = a["L1_b"].reshape(NGATE, D)
        gate_bias[row:row + NGATE, 1] = a["L3_b"].reshape(NGATE, D)
    arrays = {
        "xT_in": a["x"].transpose(2, 0, 1),
        "small_in": np.concatenate([cond.T, cond_jg.T] + [column(a[n]) for n in ("bq1", "bk1", "bq2", "bk2", "L2_b",
                                                                                 "alpha")] + [bv], axis=1),
        "wqk_in": blocks(a["Wq2"], a["Wk2"]),
        "wv_in": blocks(a["Wv"][:D], a["Wv"][D:], a["Wq1"], a["Wk1"]),
        "gate_bias_in": gate_bias,
        "wh_in": blocks(a["L1_Wh"], a["L3_Wh"], a["L2_Wh"]),
        "wx_in": blocks(a["L1_Wx"], a["L3_Wx"], a["L2_Wx"]),
    }
    arrays = {n: np.ascontiguousarray(v) for n, v in arrays.items()}
    nc = bacc.Bacc("TRN2", target_bir_lowering=False, num_devices=1)
    args = [nc.dram_tensor(n, v.shape, mybir.dt.from_np(v.dtype), kind="ExternalInput").ap()
            for n, v in arrays.items()]
    args.append(nc.dram_tensor("out", (D, S, B), mybir.dt.float32, kind="ExternalOutput").ap())
    attention_then_stacked_recurrences(nc, *args)
    r = run_bass_kernel_spmd(nc, [arrays], core_ids=[0])
    return r.results[0]["out"].transpose(2, 1, 0)
```

```python
import concourse.bass as bass
from concourse import mybir
from contextlib import ExitStack


def attention_then_stacked_recurrences(nc, xT_in, small_in, wqk_in, wv_in, gate_bias_in, wh_in, wx_in, out):
    f32, bf16, f16, i32 = mybir.dt.float32, mybir.dt.bfloat16, mybir.dt.float16, mybir.dt.int32
    ALU = mybir.AluOpType
    ACT = mybir.ActivationFunctionType
    AX = mybir.AxisListType
    RMAX = bass.bass_isa.ReduceOp.max

    D, B, S = xT_in.shape
    P = 128
    GB = P // S
    NG = B // GB
    NC = 4
    CG = NG // NC
    CT = CG * P
    CB = CG * GB
    NGATE = 4
    NP = S // 2
    PB = 2 * B
    SCALE = float(D) ** -0.5
    NW = 2 * NGATE + 1
    W1, W3, W2 = 0, NGATE, 2 * NGATE
    W_PARTS = ((W1, W3), (W3, NW))
    WARM = 8
    FIRST_TURN, LAST_TURNS = 4, (5, 4, 8)
    TOP = 14

    ctx = ExitStack()
    with ctx:
        def sb(name, shape, dt=f32):
            return ctx.enter_context(nc.sbuf_tensor(name, shape, dt))

        def sem(name):
            return ctx.enter_context(nc.semaphore(name))

        xT = sb("xT", [D, B * S])
        qT = sb("qT", [D, B * S])
        kT = sb("kT", [D, B * S])
        v_tok = sb("v_tok", [P, NG, D])
        small = sb("small", [P, 2 * B + 5 + D])
        condT = small[:, 0:B]
        condT_jg = small[:, B:2 * B]
        BQ1, BK1, BQ2, BK2, ALPHA = (small[:, 2 * B + i:2 * B + i + 1] for i in range(5))
        bv_row = small[0:1, 2 * B + 5:2 * B + 5 + D]
        wqk = sb("wqk", [D, 2, D])
        wv = sb("wv", [D, 4, D])
        ones = sb("ones", [P, P])
        table_probe = sb("table_probe", [P, 1])
        warm = sb("warm", [P, P], bf16)
        group_rows = sb("group_rows", [3 * GB, P], bf16)
        gate_cols = sb("gate_cols", [96, NGATE, PB], bf16)
        q1T, k1T, qk1 = sb("q1T", [D, B]), sb("k1T", [D, B]), sb("qk1", [D, B])
        s1, m1, d1 = sb("s1", [P, NG]), sb("m1", [P, NG]), sb("d1", [P, NG])
        e1, l1, p1 = sb("e1", [P, NG]), sb("l1", [P, NG]), sb("p1", [P, NG])
        v1_r1, v1_r2 = sb("v1_r1", [B, D]), sb("v1_r2", [B, D])
        v1_parts = sb("v1_parts", [B, 3, D], bf16)
        v1_rows = sb("v1_rows", [3 * GB, NG, D], bf16)
        sc_d, sc_e, prob = sb("sc_d", [P, NG, S]), sb("sc_e", [P, NG, S]), sb("prob", [P, NG, S])
        sc_m, sc_l = sb("sc_m", [P, NG]), sb("sc_l", [P, NG])
        probT = sb("probT", [P, NG, P])
        x_run = sb("x_run", [D, S, B])
        WX, WXs = sb("WX", [D, NW, D]), sb("WXs", [D, NW, D])
        WH, WHs = sb("WH", [D, NW, D]), sb("WHs", [D, NW, D])
        WHhi, WHlo = sb("WHhi", [D, NW, D], f16), sb("WHlo", [D, NW, D], f16)
        abs_sum, bound = sb("abs_sum", [P, 1]), sb("bound", [P, 1])
        expo, up, down = sb("expo", [P, 1], i32), sb("up", [P, 1], i32), sb("down", [P, 1], i32)
        upf = sb("upf", [P, 1], i32)
        gb_in = sb("gb_in", [96, 3, D])
        gb_r1, gb_r2 = sb("gb_r1", [96, 3, D]), sb("gb_r2", [96, 3, D])
        gb_p = sb("gb_p", [96, 3, 3, D], bf16)
        gate_bias = sb("gate_bias", [96, 3, D], bf16)

        class Lstm:
            def __init__(self, n, w0, bias, bank0):
                self.w0, self.bias = w0, bias
                self.banks = (bank0, bank0 + 1)
                self.gates = sb(f"gates{n}", [D, 3, B])
                self.g_and_c = sb(f"g_c{n}", [D, 2, B])
                self.igfc = sb(f"ig_fc{n}", [D, 2, B])
                self.c, self.tc = self.g_and_c[:, 1, :], sb(f"tc{n}", [D, B])
                self.h = sb(f"h{n}", [D, 2, B])
                self.hhi, self.hlo = sb(f"hhi{n}", [D, B], f16), sb(f"hlo{n}", [D, B], f16)
                self.pre = sem(f"preact{n}_ready")
                self.if_r, self.g_r = sem(f"if{n}_ready"), sem(f"g{n}_ready")
                self.tc_r = sem(f"tanh_c{n}_ready")
                self.ig_r, self.fc_r, self.c_r = sem(f"ig{n}_ready"), sem(f"fc{n}_ready"), sem(f"c{n}_ready")
                self.hhi_r, self.h_r, self.hlo_r = sem(f"hhi{n}_ready"), sem(f"h{n}_ready"), sem(f"hlo{n}_ready")
                self.sum_r = sem(f"x_after{n}_ready")

        bank = [ctx.enter_context(nc.psum_tensor(f"bank{i}", [P, 512], f32)) for i in range(8)]
        L1, L3 = Lstm(1, W1, 0, 0), Lstm(3, W3, 1, 2)
        RNN_BANK = 4
        h2 = sb("h2", [D, 2, B])
        h2hi, h2lo = sb("h2hi", [D, B], f16), sb("h2lo", [D, B], f16)

        SPARE_BANK = 7
        B_V1, B_SIDE, B_QK, B_V, B_S, B_O = 0, 1, (2, 3, 4), (5, 2), (6, 7), (1, 4, 6, 3)
        SIDE_Q, SIDE_K, SIDE_S = 0, B, 2 * B

        ld_x = [sem(f"ld_x{c}") for c in range(NC)]
        ld_small, ld_qk, ld_wv = sem("ld_small"), sem("ld_qk_weights"), sem("ld_v_weights")
        ld_wh, ld_wx, ld_gb = sem("ld_wh"), sem("ld_wx"), sem("ld_gate_bias")
        v1_moved, stored, warm_zero = sem("v1_moved"), sem("stored"), sem("warm_zeroed")
        table_loaded = sem("table_loaded")
        rows_zero, cols_zero = sem("group_rows_zeroed"), sem("gate_cols_zeroed")
        rows_ready, cols_ready = sem("group_rows_ready"), sem("gate_cols_ready")
        ones_ready, probT_zero = sem("ones_ready"), sem("probT_zero")
        side_mm, qk1_ready, s1_ps, s1_ready = sem("side_products"), sem("qk1_ready"), sem("s1_in_psum"), sem("s1_ready")
        m1_ready, d1_ready, e1_ready = sem("m1_ready"), sem("d1_ready"), sem("e1_ready")
        l1_ready, r1_ready, p1_ready = sem("l1_ready"), sem("r1_ready"), sem("p1_ready")
        v1_chain, v1_split = sem("v1_chain"), sem("v1_split")
        q_ps, k_ps, q_ready, k_ready = sem("q_in_psum"), sem("k_in_psum"), sem("q_ready"), sem("k_ready")
        v_ps, v_ready = sem("v_in_psum"), sem("v_ready")
        s_ps, sm_max, sm_d, sm_e = sem("scores_in_psum"), sem("max_ready"), sem("scores_less_max"), sem("exp_ready")
        sm_sum, sm_rcp, sm_2, sm_prob = sem("sum_ready"), sem("reciprocal_ready"), sem("softmax2_ready"), sem("prob_ready")
        pT_ready, o_ps = sem("probT_ready"), sem("attn_in_psum")
        x1_first, x1_ready = sem("x1_first_pair_ready"), sem("x1_ready")
        abs_ready = sem("abs_ready")
        bound_ready, scale_chain, scale_ready = sem("bound_ready"), sem("scale_chain"), sem("scale_ready")
        ws_ready, wxs_ready, whi_ready, wlo_ready = (sem("WHs_ready"), sem("WXs_ready"), sem("WHhi_ready"),
                                                     sem("WHlo_ready"))
        gb_chain, gb_ready, state_zero = sem("gate_bias_chain"), sem("gate_bias_ready"), sem("cell_state_zeroed")
        last_sum = sem("last_residual_sum")
        pre2, h2hi_r, h2_r, h2lo_r, sum2_r = (sem("preact2_ready"), sem("hhi2_ready"), sem("h2_ready"),
                                              sem("hlo2_ready"), sem("x_after2_ready"))

        def qk_bank(c, which):
            return B_QK[(2 * c + which) % 3]

        block = ctx.enter_context(nc.Block())

        @block.sync
        def _(sp):
            x_v = xT_in.rearrange("d b t -> d (b t)")
            sp.dma_start(wqk[:, :, :], wqk_in).then_inc(ld_qk, 16)
            sp.dma_start(xT[:, 0:CT], x_v[:, 0:CT]).then_inc(ld_x[0], 16)
            sp.dma_start(small[:, :], small_in).then_inc(ld_small, 16)
            sp.dma_start(wv[:, :, :], wv_in).then_inc(ld_wv, 16)
            sp.dma_start(xT[:, CT:2 * CT], x_v[:, CT:2 * CT]).then_inc(ld_x[1], 16)
            sp.dma_start(WH[:, :, :], wh_in).then_inc(ld_wh, 16)
            for c in (2, 3):
                cols = slice(c * CT, (c + 1) * CT)
                sp.dma_start(xT[:, cols], x_v[:, cols]).then_inc(ld_x[c], 16)
            sp.dma_start(gb_in[:, :, :], gate_bias_in).then_inc(ld_gb, 16)
            sp.wait_ge(v1_split, 1)
            for part in range(3):
                sp.dma_start(v1_rows[part * GB:(part + 1) * GB, :, :], v1_parts[:, part, :]).then_inc(v1_moved, 16)
            sp.dma_start(WX[:, :, :], wx_in).then_inc(ld_wx, 16)
            for p in range(NP):
                if p < NP - 1:
                    sp.wait_ge(L3.sum_r, 2 * p + 2)
                else:
                    sp.wait_ge(L3.sum_r, S - 1)
                    sp.wait_ge(last_sum, 1)
                sp.dma_start(out[:, 2 * p:2 * p + 2, :], x_run[:, 2 * p:2 * p + 2, :]).then_inc(stored, 16)
            sp.wait_ge(stored, 16 * NP)

        @block.gpsimd
        def _(pool):
            nc.gpsimd.memset(ones[:, :], 1.0).then_inc(ones_ready, 1)
            nc.gpsimd.memset(group_rows[:, :], 0.0).then_inc(rows_zero, 1)
            nc.gpsimd.memset(probT[:, :, :], 0.0).then_inc(probT_zero, 1)
            for part in range(3):
                pool.wait_ge(rows_zero, 1) if part == 0 else pool.wait_ge(rows_ready, part)
                nc.gpsimd.affine_select(out=group_rows[:, :], in_=group_rows[:, :], compare_op=ALU.not_equal,
                                        fill=1.0, base=-GB * part, pattern=[[-1, GB], [0, S]],
                                        channel_multiplier=1).then_inc(rows_ready, 1)
            nc.gpsimd.memset(gate_cols[:, :, :], 0.0).then_inc(cols_zero, 1)
            for part in range(3):
                pool.wait_ge(cols_zero, 1) if part == 0 else pool.wait_ge(cols_ready, part)
                nc.gpsimd.affine_select(out=gate_cols[:, :, :], in_=gate_cols[:, :, :], compare_op=ALU.not_equal,
                                        fill=1.0, base=-32 * part, pattern=[[-1, NGATE], [0, PB]],
                                        channel_multiplier=1).then_inc(cols_ready, 1)
            pool.wait_ge(abs_ready, 1)
            nc.gpsimd.partition_all_reduce(bound[:, :], abs_sum[:, :], P, RMAX).then_inc(bound_ready, 1)
            pool.wait_ge(ld_gb, 16)
            nc.gpsimd.tensor_copy(gb_p[:, 0, :, :], gb_in[:, :, :]).then_inc(gb_chain, 1)
            pool.wait_ge(gb_chain, 1)
            nc.gpsimd.tensor_tensor(gb_r1[:, :, :], gb_in[:, :, :], gb_p[:, 0, :, :], ALU.subtract).then_inc(gb_chain, 1)
            pool.wait_ge(gb_chain, 2)
            nc.gpsimd.tensor_copy(gb_p[:, 1, :, :], gb_r1[:, :, :]).then_inc(gb_chain, 1)
            pool.wait_ge(gb_chain, 3)
            nc.gpsimd.tensor_tensor(gb_r2[:, :, :], gb_r1[:, :, :], gb_p[:, 1, :, :], ALU.subtract).then_inc(gb_chain, 1)
            pool.wait_ge(gb_chain, 4)
            nc.gpsimd.tensor_copy(gb_p[:, 2, :, :], gb_r2[:, :, :]).then_inc(gb_chain, 1)
            def weights_low(n):
                lo, hi = W_PARTS[n]
                pool.wait_ge(ws_ready, n + 1)
                pool.wait_ge(whi_ready, n + 1)
                nc.gpsimd.tensor_tensor(WHlo[:, lo:hi, :], WHs[:, lo:hi, :], WHhi[:, lo:hi, :],
                                        ALU.subtract).then_inc(wlo_ready, 1)

            weights_low(0)

            def sum1(t):
                pool.wait_ge(L1.h_r, t + 1)
                nc.gpsimd.tensor_tensor(x_run[:, t, :], x_run[:, t, :], L1.h[:, t % 2, :],
                                        ALU.add).then_inc(L1.sum_r, 1)

            def sum3(t):
                pool.wait_ge(L3.h_r, t + 1)
                nc.gpsimd.tensor_tensor(x_run[:, t, :], x_run[:, t, :], L3.h[:, t % 2, :],
                                        ALU.add).then_inc(L3.sum_r, 1)

            def kept_cell(L, t):
                pool.wait_ge(L.if_r, t + 1)
                if t == 0:
                    pool.wait_ge(state_zero, 2)
                nc.gpsimd.tensor_tensor(L.igfc[:, 1, :], L.gates[:, 1, :], L.c, ALU.mult).then_inc(L.fc_r, 1)

            for k in range(NP + 2):
                if k < NP:
                    kept_cell(L1, 2 * k)
                if k == 0:
                    weights_low(1)
                if k >= 3:
                    sum3(2 * (k - 3) + 1)
                if 2 <= k <= NP + 1:
                    kept_cell(L3, 2 * (k - 2) + 1)
                if k < NP:
                    kept_cell(L1, 2 * k + 1)
                    sum1(2 * k)
                if 2 <= k <= NP + 1:
                    sum3(2 * (k - 2))
                if 1 <= k <= NP:
                    kept_cell(L3, 2 * (k - 1))
                if k < NP:
                    sum1(2 * k + 1)

        @block.scalar
        def _(act):
            act.wait_ge(warm_zero, 1)
            nc.scalar.activation(table_probe[:, :], warm[:, 0:1], ACT.Exp).then_inc(table_loaded, 1)

            def exp_of(c):
                g = slice(c * CG, (c + 1) * CG)
                act.wait_ge(sm_d, c + 1)
                nc.scalar.activation(sc_e[:, g, :], sc_d[:, g, :], ACT.Exp, scale=SCALE).then_inc(sm_e, 1)

            def q_out(c):
                act.wait_ge(q_ps, c + 1)
                nc.scalar.activation(qT[:, c * CT:(c + 1) * CT], bank[qk_bank(c, 0)][:, :], ACT.Identity,
                                     bias=BQ2).then_inc(q_ready, 1)

            def k_out(c):
                act.wait_ge(k_ps, c + 1)
                nc.scalar.activation(kT[:, c * CT:(c + 1) * CT], bank[qk_bank(c, 1)][:, :], ACT.Identity,
                                     bias=BK2).then_inc(k_ready, 1)

            def v_out(c):
                act.wait_ge(v_ps, c + 1)
                nc.scalar.activation(v_tok[:, c * CG:(c + 1) * CG, :],
                                     bank[B_V[c % 2]][:, :].rearrange("p (g d) -> p g d", d=D),
                                     ACT.Copy).then_inc(v_ready, 1)

            def scaled(dst, src, part, done):
                lo, hi = W_PARTS[part]
                nc.scalar.activation(dst[:, lo:hi, :], src[:, lo:hi, :], ACT.Copy,
                                     scale=upf[:, 0:1].bitcast(f32)).then_inc(done, 1)

            def scaled_bias(part):
                q = slice(32 * part, 32 * part + 32)
                nc.scalar.activation(gate_bias[q, :, :], gb_p[q, part, :, :], ACT.Copy,
                                     scale=upf[q, 0:1].bitcast(f32)).then_inc(gb_ready, 1)

            act.wait_ge(ld_small, 16)
            q_out(0)
            k_out(0)
            act.wait_ge(ld_wh, 16)
            nc.scalar.activation(WHs[:, :, :], WH[:, :, :], ACT.Abs, accum_out=abs_sum[:, :]).then_inc(abs_ready, 1)
            q_out(1)
            k_out(1)
            exp_of(0)
            q_out(2)
            k_out(2)
            act.wait_ge(d1_ready, 1)
            nc.scalar.activation(e1[:, :], d1[:, :], ACT.Exp, scale=SCALE).then_inc(e1_ready, 1)
            exp_of(1)
            q_out(3)
            k_out(3)
            v_out(0)
            exp_of(2)
            act.wait_ge(scale_ready, 1)
            scaled(WHs, WH, 0, ws_ready)
            scaled(WHhi, WH, 0, whi_ready)
            v_out(1)
            act.wait_ge(gb_chain, 5)
            scaled_bias(0)
            exp_of(3)
            act.wait_ge(table_loaded, 1)
            nc.scalar.activation(table_probe[:, :], warm[:, 0:1], ACT.Sigmoid).then_inc(table_loaded, 1)
            v_out(2)
            scaled_bias(1)
            scaled_bias(2)
            v_out(3)
            act.wait_ge(ld_wx, 16)
            scaled(WXs, WX, 0, wxs_ready)
            scaled(WHs, WH, 1, ws_ready)
            scaled(WHhi, WH, 1, whi_ready)
            scaled(WXs, WX, 1, wxs_ready)
            unscale = act.alloc_register("unscale")
            act.reg_load(unscale, down[0:1, 0:1])

            def pair_cols(bk, g0, g1, s):
                return bank[bk][:, :].rearrange("p (g s b) -> p g s b", g=NGATE, s=2)[:, g0:g1, s, :]

            def i_f_g(L, t):
                bk, s = L.banks[(t // 2) % 2], t % 2
                act.wait_ge(L.pre, t + 1)
                nc.scalar.activation(L.gates[:, 0:2, :], pair_cols(bk, 0, 2, s), ACT.Sigmoid,
                                     scale=unscale).then_inc(L.if_r, 1)
                nc.scalar.activation(L.g_and_c[:, 0:1, :], pair_cols(bk, 3, 4, s), ACT.Tanh,
                                     scale=unscale).then_inc(L.g_r, 1)

            def o(L, t):
                bk, s = L.banks[(t // 2) % 2], t % 2
                nc.scalar.activation(L.gates[:, 2:3, :], pair_cols(bk, 2, 3, s), ACT.Sigmoid, scale=unscale)

            def rnn_cols(t):
                return bank[RNN_BANK + (t // 2) % 2][:, (t % 2) * B:(t % 2 + 1) * B]

            def tanh_c(L, t):
                act.wait_ge(L.c_r, t + 1)
                nc.scalar.activation(L.tc[:, :], L.c, ACT.Tanh).then_inc(L.tc_r, 1)

            def rnn(t):
                act.wait_ge(pre2, t + 1)
                if t >= 2:
                    act.wait_ge(sum2_r, t - 1)
                nc.scalar.activation(h2[:, t % 2, :], rnn_cols(t), ACT.Tanh, scale=unscale).then_inc(h2_r, 1)

            def rnn_high(t):
                nc.scalar.activation(h2hi[:, :], rnn_cols(t), ACT.Tanh, scale=unscale).then_inc(h2hi_r, 1)

            for k in range(NP + 2):
                in1, in2, in3 = k < NP, 1 <= k <= NP, k >= 2
                if in1:
                    i_f_g(L1, 2 * k)
                if in2:
                    rnn(2 * (k - 1))
                    rnn_high(2 * (k - 1))
                if in1:
                    o(L1, 2 * k)
                    tanh_c(L1, 2 * k)
                if in3:
                    i_f_g(L3, 2 * (k - 2) + 1)
                if in2:
                    rnn(2 * (k - 1) + 1)
                if in3:
                    o(L3, 2 * (k - 2) + 1)
                if in2:
                    rnn_high(2 * (k - 1) + 1)
                if in3:
                    tanh_c(L3, 2 * (k - 2) + 1)
                if in1:
                    i_f_g(L1, 2 * k + 1)
                    o(L1, 2 * k + 1)
                    tanh_c(L1, 2 * k + 1)
                if in2:
                    i_f_g(L3, 2 * (k - 1))
                    o(L3, 2 * (k - 1))
                    tanh_c(L3, 2 * (k - 1))

        @block.vector
        def _(dve):
            nc.vector.memset(warm[:, :], 0.0).then_inc(warm_zero, 1)
            for L in (L1, L3):
                nc.vector.memset(L.c, 0.0).then_inc(state_zero, 1)

            def row_max(c):
                g = slice(c * CG, (c + 1) * CG)
                dve.wait_ge(s_ps, c + 1)
                nc.vector.tensor_reduce(sc_m[:, g], bank[B_S[c % 2]][:, 0:CG * S].rearrange("p (g k) -> p g k", k=S),
                                        axis=AX.X, op=ALU.max).then_inc(sm_max, 1)

            def less_max(c):
                g = slice(c * CG, (c + 1) * CG)
                dve.wait_ge(sm_max, c + 1)
                nc.vector.tensor_tensor(sc_d[:, g, :], bank[B_S[c % 2]][:, 0:CG * S].rearrange("p (g k) -> p g k", k=S),
                                        sc_m[:, g].unsqueeze(2).to_broadcast([P, CG, S]),
                                        ALU.subtract).then_inc(sm_d, 1)

            def row_sum(c):
                g = slice(c * CG, (c + 1) * CG)
                dve.wait_ge(sm_e, c + 1)
                nc.vector.tensor_reduce(sc_l[:, g], sc_e[:, g, :], axis=AX.X, op=ALU.add).then_inc(sm_sum, 1)

            def reciprocal(c):
                g = slice(c * CG, (c + 1) * CG)
                dve.wait_ge(sm_sum, c + 1)
                nc.vector.reciprocal(sc_m[:, g], sc_l[:, g]).then_inc(sm_rcp, 1)

            def over_sum(c):
                g = slice(c * CG, (c + 1) * CG)
                dve.wait_ge(sm_rcp, c + 1)
                nc.vector.tensor_tensor(sc_d[:, g, :], sc_e[:, g, :],
                                        sc_m[:, g].unsqueeze(2).to_broadcast([P, CG, S]),
                                        ALU.mult).then_inc(sm_2, 1)

            def less_first(c):
                g = slice(c * CG, (c + 1) * CG)
                dve.wait_ge(sm_2, c + 1)
                if c == 0:
                    dve.wait_ge(p1_ready, 1)
                nc.vector.tensor_tensor(prob[:, g, :], sc_d[:, g, :],
                                        p1[:, g].unsqueeze(2).to_broadcast([P, CG, S]),
                                        ALU.subtract).then_inc(sm_prob, 1)

            def transposed(c, js):
                g = slice(c * CG, (c + 1) * CG)
                dve.wait_ge(sm_prob, c + 1)
                if c == 0:
                    dve.wait_ge(probT_zero, 1)
                for j in js:
                    q = slice(j * S, (j + 1) * S)
                    nc.vector.transpose(probT[q, g, q], prob[q, g, :]).then_inc(pT_ready, 1)

            def residual(c, steps, done):
                if steps.start == 0:
                    dve.wait_ge(o_ps, c + 1)
                nc.vector.tensor_tensor(x_run[:, steps, c * CB:(c + 1) * CB].rearrange("p t b -> p b t"),
                                        bank[B_O[c]][:, :].rearrange("p (b t) -> p b t", t=S)[:, :, steps],
                                        xT[:, c * CT:(c + 1) * CT].rearrange("p (b t) -> p b t", t=S)[:, :, steps],
                                        ALU.add).then_inc(done, 1)

            def first_softmax_start():
                dve.wait_ge(s1_ready, 1)
                nc.vector.tensor_reduce(m1[:, :], s1[:, :].unsqueeze(2).to_broadcast([P, NG, S]), axis=AX.X,
                                        op=ALU.max).then_inc(m1_ready, 1)

            def first_softmax_less_max():
                dve.wait_ge(m1_ready, 1)
                nc.vector.tensor_tensor(d1[:, :], s1[:, :], m1[:, :], ALU.subtract).then_inc(d1_ready, 1)

            def first_softmax_sum():
                dve.wait_ge(e1_ready, 1)
                nc.vector.tensor_reduce(l1[:, :], e1[:, :].unsqueeze(2).to_broadcast([P, NG, S]), axis=AX.X,
                                        op=ALU.add).then_inc(l1_ready, 1)

            def first_softmax_reciprocal():
                dve.wait_ge(l1_ready, 1)
                nc.vector.reciprocal(m1[:, :], l1[:, :]).then_inc(r1_ready, 1)

            def first_softmax_end():
                dve.wait_ge(r1_ready, 1)
                nc.vector.scalar_tensor_tensor(out=p1[:, :], in0=m1[:, :], scalar=ALPHA, in1=e1[:, :],
                                               op0=ALU.mult, op1=ALU.mult).then_inc(p1_ready, 1)

            def scale_step(n):
                if n == 0:
                    dve.wait_ge(bound_ready, 1)
                else:
                    dve.wait_ge(scale_chain, min(n, 3) if n < 5 else 5)
                if n == 0:
                    nc.vector.tensor_scalar(expo[:, :], bound[:, :].bitcast(i32), 23, None,
                                            ALU.logical_shift_right).then_inc(scale_chain, 1)
                elif n == 1:
                    nc.vector.tensor_scalar(up[:, :], expo[:, :], -1, 254 + TOP, ALU.mult,
                                            ALU.add).then_inc(scale_chain, 1)
                elif n == 2:
                    nc.vector.tensor_scalar(up[:, :], up[:, :], 127 + 2 * TOP, None, ALU.min).then_inc(scale_chain, 1)
                elif n == 3:
                    nc.vector.tensor_scalar(expo[:, :], up[:, :], -1, 254, ALU.mult, ALU.add).then_inc(scale_chain, 1)
                    nc.vector.tensor_scalar(upf[:, :], up[:, :], 23, None,
                                            ALU.logical_shift_left).then_inc(scale_chain, 1)
                else:
                    nc.vector.tensor_scalar(down[:, :], expo[:, :], 23, None,
                                            ALU.logical_shift_left).then_inc(scale_ready, 1)

            dve.wait_ge(side_mm, 1)
            v1_ps = bank[B_V1][0:B, 0:D]
            nc.vector.tensor_copy(v1_parts[:, 0, :], v1_ps).then_inc(v1_chain, 1)
            dve.wait_ge(v1_chain, 1)
            nc.vector.tensor_tensor(v1_r1[:, :], v1_ps, v1_parts[:, 0, :], ALU.subtract).then_inc(v1_chain, 1)
            dve.wait_ge(v1_chain, 2)
            nc.vector.tensor_copy(v1_parts[:, 1, :], v1_r1[:, :]).then_inc(v1_chain, 1)
            dve.wait_ge(v1_chain, 3)
            nc.vector.tensor_tensor(v1_r2[:, :], v1_r1[:, :], v1_parts[:, 1, :], ALU.subtract).then_inc(v1_chain, 1)
            dve.wait_ge(v1_chain, 4)
            nc.vector.tensor_copy(v1_parts[:, 2, :], v1_r2[:, :]).then_inc(v1_split, 1)
            dve.wait_ge(side_mm, 2)
            dve.wait_ge(ld_small, 16)
            nc.vector.tensor_scalar(q1T[:, :], bank[B_SIDE][:, SIDE_Q:SIDE_Q + B], BQ1, None,
                                    ALU.add).then_inc(qk1_ready, 1)
            nc.vector.tensor_scalar(k1T[:, :], bank[B_SIDE][:, SIDE_K:SIDE_K + B], BK1, None,
                                    ALU.add).then_inc(qk1_ready, 1)
            dve.wait_ge(qk1_ready, 2)
            nc.vector.tensor_tensor(qk1[:, :], q1T[:, :], k1T[:, :], ALU.mult).then_inc(qk1_ready, 1)
            row_max(0)
            less_max(0)
            dve.wait_ge(s1_ps, 1)
            nc.vector.tensor_copy(s1[:, :], bank[B_SIDE][:, SIDE_S:SIDE_S + NG]).then_inc(s1_ready, 1)
            row_sum(0)
            first_softmax_start()
            reciprocal(0)
            first_softmax_less_max()
            scale_step(0)
            row_max(1)
            scale_step(1)
            over_sum(0)
            scale_step(2)
            less_max(1)
            first_softmax_sum()
            scale_step(3)
            first_softmax_reciprocal()
            scale_step(5)
            first_softmax_end()
            row_max(2)
            less_first(0)
            row_sum(1)
            transposed(0, range(0, 2))
            less_max(2)
            transposed(0, range(2, GB))
            reciprocal(1)
            over_sum(1)
            row_sum(2)
            less_first(1)
            reciprocal(2)
            transposed(1, range(GB))
            row_max(3)
            over_sum(2)
            less_max(3)
            less_first(2)
            residual(0, slice(0, S), x1_ready)
            transposed(2, range(0, 2))
            row_sum(3)
            transposed(2, range(2, 3))
            reciprocal(3)
            transposed(2, range(3, GB))
            over_sum(3)
            less_first(3)
            transposed(3, range(GB))
            residual(1, slice(0, S), x1_ready)
            residual(2, slice(0, 2), x1_first)
            residual(3, slice(0, 2), x1_first)
            residual(2, slice(2, S), x1_ready)
            residual(3, slice(2, S), x1_ready)

            def cell_terms(L, t):
                dve.wait_ge(L.g_r, t + 1)
                nc.vector.tensor_tensor(L.igfc[:, 0, :], L.gates[:, 0, :], L.g_and_c[:, 0, :], ALU.mult).then_inc(L.ig_r, 1)

            def cell(L, t):
                dve.wait_ge(L.ig_r, t + 1)
                dve.wait_ge(L.fc_r, t + 1)
                nc.vector.tensor_tensor(L.c, L.igfc[:, 0, :], L.igfc[:, 1, :], ALU.add).then_inc(L.c_r, 1)

            def hidden(L, t):
                dve.wait_ge(L.tc_r, t + 1)
                if t < S - 1:
                    nc.vector.tensor_tensor(L.hhi[:, :], L.gates[:, 2, :], L.tc[:, :], ALU.mult).then_inc(L.hhi_r, 1)
                if t >= 2:
                    dve.wait_ge(L.sum_r, t - 1)
                nc.vector.tensor_tensor(L.h[:, t % 2, :], L.gates[:, 2, :], L.tc[:, :], ALU.mult).then_inc(L.h_r, 1)

            def rnn_split(t):
                dve.wait_ge(h2hi_r, t + 1)
                nc.vector.tensor_tensor(h2lo[:, :], h2[:, t % 2, :], h2hi[:, :], ALU.subtract).then_inc(h2lo_r, 1)

            def sum2(t):
                dve.wait_ge(h2_r, t + 1)
                nc.vector.tensor_tensor(x_run[:, t, :], x_run[:, t, :], h2[:, t % 2, :],
                                        ALU.add).then_inc(sum2_r, 1)

            def hidden_low(L, t):
                dve.wait_ge(L.h_r, t + 1)
                nc.vector.tensor_tensor(L.hlo[:, :], L.h[:, t % 2, :], L.hhi[:, :], ALU.subtract).then_inc(L.hlo_r, 1)

            for k in range(NP + 2):
                in1, next1, in2, in3 = k < NP, k + 1 < NP, 1 <= k <= NP, k >= 2
                if in1:
                    cell_terms(L1, 2 * k)
                if in3:
                    hidden_low(L3, 2 * (k - 2))
                if in1:
                    cell(L1, 2 * k)
                if in2:
                    rnn_split(2 * (k - 1))
                    sum2(2 * (k - 1))
                if in1:
                    hidden(L1, 2 * k)
                if in3:
                    cell_terms(L3, 2 * (k - 2) + 1)
                if in1:
                    hidden_low(L1, 2 * k)
                if in2:
                    sum2(2 * (k - 1) + 1)
                if in3:
                    cell(L3, 2 * (k - 2) + 1)
                    hidden(L3, 2 * (k - 2) + 1)
                if in1:
                    cell_terms(L1, 2 * k + 1)
                if 2 <= k <= NP:
                    hidden_low(L3, 2 * (k - 2) + 1)
                if in1:
                    cell(L1, 2 * k + 1)
                if in2:
                    rnn_split(2 * (k - 1) + 1)
                if in1:
                    hidden(L1, 2 * k + 1)
                if in2:
                    cell_terms(L3, 2 * (k - 1))
                if next1:
                    hidden_low(L1, 2 * k + 1)
                if in2:
                    cell(L3, 2 * (k - 1))
                    hidden(L3, 2 * (k - 1))
            dve.wait_ge(L3.h_r, S)
            nc.vector.tensor_tensor(x_run[:, S - 1, :], x_run[:, S - 1, :], L3.h[:, (S - 1) % 2, :],
                                    ALU.add).then_inc(last_sum, 1)

        @block.tensor
        def _(pe):
            mm = nc.tensor.matmul

            def project_qk(c):
                cols = slice(c * CT, (c + 1) * CT)
                pe.wait_ge(ld_x[c], 16)
                if c == 0:
                    pe.wait_ge(ld_qk, 16)
                for which, done in enumerate((q_ps, k_ps)):
                    n = 2 * c + which - 3
                    if n >= 0:
                        pe.wait_ge((q_ready, k_ready)[n % 2], n // 2 + 1)
                    mm(bank[qk_bank(c, which)][:, :], wqk[:, which, :], xT[:, cols],
                       start=True, stop=True).then_inc(done, 1)

            def project_v(c):
                if c >= 2:
                    pe.wait_ge(v_ready, c - 1)
                elif c == 1:
                    pe.wait_ge(q_ready, NC)
                for g in range(CG):
                    mm(bank[B_V[c % 2]][:, g * D:(g + 1) * D], xT[:, c * CT + g * P:c * CT + (g + 1) * P], wv[:, 1, :],
                       start=g == 0, stop=False, skip_group_check=True)
                if c == 0:
                    pe.wait_ge(rows_ready, 3)
                    pe.wait_ge(v1_moved, 16 * 3)
                mm(bank[B_V[c % 2]][:, :], group_rows[:, :],
                   v1_rows[:, c * CG:(c + 1) * CG, :].rearrange("r g d -> r (g d)"),
                   start=False, stop=True, skip_group_check=True).then_inc(v_ps, 1)

            def scores(c):
                pe.wait_ge(q_ready, c + 1)
                pe.wait_ge(k_ready, c + 1)
                if c >= 2:
                    pe.wait_ge(sm_d, c - 1)
                for g in range(CG):
                    for j in range(GB):
                        tok = slice((c * CB + g * GB + j) * S, (c * CB + g * GB + j + 1) * S)
                        last = mm(bank[B_S[c % 2]][j * S:(j + 1) * S, g * S:(g + 1) * S], qT[:, tok], kT[:, tok],
                                  start=True, stop=True)
                last.then_inc(s_ps, 1)

            def attend(c):
                pe.wait_ge(pT_ready, GB * (c + 1))
                pe.wait_ge(v_ready, c + 1)
                if c == 1:
                    pe.wait_ge(k_ready, NC - 1)
                if c == 3:
                    pe.wait_ge(k_ready, NC)
                for g in range(CG):
                    last = mm(bank[B_O[c]][:, g * P:(g + 1) * P], v_tok[:, c * CG + g, :], probT[:, c * CG + g, :],
                              start=True, stop=True)
                last.then_inc(o_ps, 1)

            def side_products():
                pe.wait_ge(ld_small, 16)
                pe.wait_ge(ones_ready, 1)
                pe.wait_ge(ld_wv, 16)
                mm(bank[B_V1][0:B, 0:D], condT_jg, wv[:, 0, :], start=True, stop=False)
                mm(bank[B_V1][0:B, 0:D], ones[0:1, 0:B], bv_row, start=False, stop=True).then_inc(side_mm, 1)
                mm(bank[B_SIDE][:, SIDE_Q:SIDE_Q + B], wv[:, 2, :], condT_jg, start=True, stop=True)
                mm(bank[B_SIDE][:, SIDE_K:SIDE_K + B], wv[:, 3, :], condT_jg, start=True,
                   stop=True).then_inc(side_mm, 1)

            def side_scores():
                pe.wait_ge(qk1_ready, 3)
                for j in range(GB):
                    last = mm(bank[B_SIDE][j * S:(j + 1) * S, SIDE_S:SIDE_S + NG], ones[:, 0:S],
                              qk1[:, j * NG:(j + 1) * NG],
                              start=True, stop=True)
                last.then_inc(s1_ps, 1)

            def bias_half(L, p, half):
                g = slice(2 * half, 2 * half + 2)
                mm(bank[L.banks[p % 2]][:, 2 * half * PB:(2 * half + 2) * PB], gate_bias[:, L.bias, :],
                   gate_cols[:, g, :].rearrange("r g n -> r (g n)"),
                   start=half == 0, stop=False, skip_group_check=True)

            def gates_from_x(L, p, gates):
                for g in gates:
                    last = mm(bank[L.banks[p % 2]][:, g * PB:(g + 1) * PB], WXs[:, L.w0 + g, :], x_of(p),
                              start=False, stop=False, skip_group_check=True)
                return last

            def high_product(ps, w, hhi, hhi_r, t, gates):
                pe.wait_ge(hhi_r, t)
                for g in gates:
                    for part in (WHhi, WHlo):
                        mm(ps(g), part[:, w + g, :], hhi[:, :], start=False, stop=False, skip_group_check=True)

            def low_product(ps, w, hlo, hlo_r, t, gates):
                pe.wait_ge(hlo_r, t)
                for g in gates:
                    last = mm(ps(g), WHhi[:, w + g, :], hlo[:, :], start=False, stop=True, skip_group_check=True)
                return last

            def first_product(ps, w, gates):
                for g in gates:
                    mm(ps(g), WHs[:, w + g, :], condT, start=False, stop=False, skip_group_check=True)

            def gate_columns(L, t):
                bk, s = bank[L.banks[(t // 2) % 2]], t % 2
                return lambda g: bk[:, g * PB + s * B:g * PB + (s + 1) * B]

            GATES = (1, 0, 3, 2)

            def lstm_high(L, t):
                high_product(gate_columns(L, t), L.w0, L.hhi, L.hhi_r, t, GATES)

            def lstm_low(L, t):
                low_product(gate_columns(L, t), L.w0, L.hlo, L.hlo_r, t, GATES).then_inc(L.pre, 1)

            def x_of(p):
                return x_run[:, 2 * p:2 * p + 2, :].rearrange("d s b -> d (s b)")

            def rnn_bias(p):
                mm(bank[RNN_BANK + p % 2][:, 0:PB], gate_bias[:, 2, :], gate_cols[:, 0, :],
                   start=True, stop=False, skip_group_check=True)

            def rnn_x(p):
                pe.wait_ge(L1.sum_r, 2 * p + 2)
                return mm(bank[RNN_BANK + p % 2][:, 0:PB], WXs[:, W2, :], x_of(p),
                          start=False, stop=False, skip_group_check=True)

            def rnn_columns(t):
                return lambda g: bank[RNN_BANK + (t // 2) % 2][:, (t % 2) * B:(t % 2 + 1) * B]

            def rnn_high(t):
                high_product(rnn_columns(t), W2, h2hi, h2hi_r, t, (0,))

            def rnn_low(t):
                low_product(rnn_columns(t), W2, h2lo, h2lo_r, t, (0,)).then_inc(pre2, 1)

            def keep_clock(n):
                for _ in range(n):
                    mm(bank[SPARE_BANK][:, :], warm[:, :], warm[:, :].unsqueeze(1).to_broadcast([P, 4, P]),
                       start=True, stop=True)

            pe.wait_ge(warm_zero, 1)
            keep_clock(WARM)
            project_qk(0)
            side_products()
            project_qk(1)
            scores(0)
            side_scores()
            project_qk(2)
            scores(1)
            project_qk(3)
            scores(2)
            project_v(0)
            scores(3)
            project_v(1)
            attend(0)
            project_v(2)
            attend(1)
            project_v(3)
            attend(2)
            pe.wait_ge(gb_ready, 3)
            pe.wait_ge(cols_ready, 3)
            pe.wait_ge(v1_split, 1)
            bias_half(L1, 0, 0)
            bias_half(L1, 0, 1)
            pe.wait_ge(ws_ready, 1)
            first_product(gate_columns(L1, 0), L1.w0, (0,))
            attend(3)
            first_product(gate_columns(L1, 0), L1.w0, (1, 2, 3))
            pe.wait_ge(wxs_ready, 1)
            pe.wait_ge(x1_first, 2)
            pe.wait_ge(x1_ready, NC - 2)
            gates_from_x(L1, 0, range(NGATE)).then_inc(L1.pre, 1)
            for k in range(NP + 2):
                in1, next1, in2, in3 = k < NP, k + 1 < NP, 1 <= k <= NP, k >= 2
                if k == 0:
                    pe.wait_ge(x1_ready, NC)
                    pe.wait_ge(wlo_ready, 1)
                if k == 1:
                    pe.wait_ge(wlo_ready, len(W_PARTS))
                    pe.wait_ge(wxs_ready, len(W_PARTS))
                if 0 < k < NP:
                    lstm_high(L1, 2 * k)
                if 2 <= k <= NP:
                    rnn_bias(k - 1)
                    rnn_high(2 * (k - 1))
                if 0 < k < NP:
                    lstm_low(L1, 2 * k)
                if next1:
                    bias_half(L1, k + 1, 0)
                if k == NP:
                    keep_clock(LAST_TURNS[0])
                if k == 1:
                    rnn_x(0).then_inc(pre2, 1)
                if 2 <= k <= NP:
                    rnn_x(k - 1)
                    rnn_low(2 * (k - 1))
                    bias_half(L3, k - 1, 0)
                if next1:
                    gates_from_x(L1, k + 1, (0,))
                if in3:
                    lstm_high(L3, 2 * (k - 2) + 1)
                    lstm_low(L3, 2 * (k - 2) + 1)
                if in2:
                    rnn_high(2 * (k - 1) + 1)
                if next1:
                    gates_from_x(L1, k + 1, (1,))
                if 2 <= k <= NP:
                    bias_half(L3, k - 1, 1)
                if in2:
                    rnn_low(2 * (k - 1) + 1)
                if next1:
                    gates_from_x(L1, k + 1, (2,))
                if k == 0:
                    keep_clock(FIRST_TURN)
                if k == NP:
                    keep_clock(LAST_TURNS[1])
                if in1:
                    lstm_high(L1, 2 * k + 1)
                if next1:
                    bias_half(L1, k + 1, 1)
                if in1:
                    lstm_low(L1, 2 * k + 1)
                if in2:
                    pe.wait_ge(sum2_r, 2 * (k - 1) + 2)
                    x_products = gates_from_x(L3, k - 1, range(NGATE))
                if k == 1:
                    x_products.then_inc(L3.pre, 1)
                elif in2:
                    lstm_high(L3, 2 * (k - 1))
                    lstm_low(L3, 2 * (k - 1))
                if next1:
                    gates_from_x(L1, k + 1, (3,))
                if k == 0:
                    pe.wait_ge(ws_ready, len(W_PARTS))
                    bias_half(L3, 0, 0)
                    bias_half(L3, 0, 1)
                    first_product(gate_columns(L3, 0), L3.w0, range(NGATE))
                    rnn_bias(0)
                    first_product(rnn_columns(0), W2, (0,))
                if k == NP:
                    keep_clock(LAST_TURNS[2])

def kernel(**inputs):
    import numpy as np
    import concourse.bacc as bacc
    from concourse.bass_utils import run_bass_kernel_spmd

    a = {name.replace("L0_cond_", "").replace("_cond_", "_"): np.asarray(v) for name, v in inputs.items()}
    cond = a["cond_1024"]
    B, D = cond.shape
    S = a["x"].shape[1]
    GB, NGATE = 128 // S, 4

    def column(v):
        return np.broadcast_to(v.reshape(-1, 1), (D, 1))

    def blocks(*ws):
        return np.concatenate([w.reshape(D, -1, D) for w in ws], axis=1)

    cond_jg = cond.reshape(B // GB, GB, D).transpose(1, 0, 2).reshape(B, D)
    bv = np.zeros((D, D), a["bv"].dtype)
    bv[0] = a["bv"]
    gate_bias = np.zeros((96, 3, D), a["L1_b"].dtype)
    for row in range(0, 96, 32):
        gate_bias[row:row + NGATE, 0] = a["L1_b"].reshape(NGATE, D)
        gate_bias[row:row + NGATE, 1] = a["L3_b"].reshape(NGATE, D)
        gate_bias[row, 2] = a["L2_b"]
    arrays = {
        "xT_in": a["x"].transpose(2, 0, 1),
        "small_in": np.concatenate([cond.T, cond_jg.T] + [column(a[n]) for n in ("bq1", "bk1", "bq2", "bk2", "alpha")] + [bv], axis=1),
        "wqk_in": blocks(a["Wq2"], a["Wk2"]),
        "wv_in": blocks(a["Wv"][:D], a["Wv"][D:], a["Wq1"], a["Wk1"]),
        "gate_bias_in": gate_bias,
        "wh_in": blocks(a["L1_Wh"], a["L3_Wh"], a["L2_Wh"]),
        "wx_in": blocks(a["L1_Wx"], a["L3_Wx"], a["L2_Wx"]),
    }
    arrays = {n: np.ascontiguousarray(v) for n, v in arrays.items()}
    nc = bacc.Bacc("TRN2", target_bir_lowering=False, num_devices=1)
    args = [nc.dram_tensor(n, v.shape, mybir.dt.from_np(v.dtype), kind="ExternalInput").ap()
            for n, v in arrays.items()]
    args.append(nc.dram_tensor("out", (D, S, B), mybir.dt.float32, kind="ExternalOutput").ap())
    attention_then_stacked_recurrences(nc, *args)
    r = run_bass_kernel_spmd(nc, [arrays], core_ids=[0])
    return r.results[0]["out"].transpose(2, 1, 0)
```
